# Optimizing a Trainium2 kernel written in Bass

```python
import numpy as np
import jax
import jax.numpy as jnp

def _softmax(x, axis=-1):
    return jax.nn.softmax(x, axis=axis)

def _gelu(x):
    return jax.nn.gelu(x, approximate=True)

def _silu(x):
    return jax.nn.silu(x)

def _sigmoid(x):
    return jax.nn.sigmoid(x)

def _layernorm(x, axis=-1, eps=1e-05):
    m = jnp.mean(x, axis=axis, keepdims=True)
    v = jnp.var(x, axis=axis, keepdims=True)
    return (x - m) / jnp.sqrt(v + eps)

def _scatter_add(tgt, idx, src, axis=0):
    return tgt.at[idx].add(src)

def _segment_sum(src, seg, n):
    return jax.ops.segment_sum(src, seg, n)
kernel_name = 'mk_gnn_preln_d4_gnn_r64_111ab1'

def setup_inputs(seed: int=0):
    np.random.seed(seed)
    _w = jnp.asarray

    def _rec_inputs():
        import jax
        import jax.numpy as jnp
        _gk = jax.random.key(seed)
        x = -0.000202 + 1 * jax.random.normal(jax.random.fold_in(_gk, 1), (100000, 64), jnp.float32)
        src = jax.random.randint(jax.random.fold_in(_gk, 2), (50000,), 0, 100000, jnp.int32)
        dst = jax.random.randint(jax.random.fold_in(_gk, 3), (50000,), 0, 100000, jnp.int32)
        _o = jnp.argsort(dst, stable=True)
        src = src[_o]
        dst = dst[_o]
        edge_type_16 = jax.random.randint(jax.random.fold_in(_gk, 13), (50000,), 0, 16, jnp.int32)
        return (x, src, dst, edge_type_16)
    x, src, dst, edge_type_16 = _rec_inputs()

    def _L0_gnn_setup():
        import jax, jax.numpy as jnp
        import numpy as np
        N_NODES = 100000
        N_EDGES = 15625
        D_IN = 64
        D_OUT = 64
        N_RELS = 16
        key = jax.random.key(seed)
        k1, k2, k3, k4, k5 = jax.random.split(key, 5)
        feat = jax.random.normal(k1, (N_NODES, D_IN), dtype=jnp.float32)
        weight = jax.random.normal(k2, (N_RELS, D_IN, D_OUT), dtype=jnp.float32) * 0.05
        src = jax.random.randint(k3, (N_EDGES,), 0, N_NODES)
        dst = jax.random.randint(k4, (N_EDGES,), 0, N_NODES)
        etypes = jax.random.randint(k5, (N_EDGES,), 0, N_RELS)
        return {'feat': feat, 'weight': weight, 'src': src, 'dst': dst, 'etypes': etypes}
    _L0_gnn_all = _L0_gnn_setup()
    _L0_gnn_in = {k: v for k, v in _L0_gnn_all.items() if k in ('weight',)}
    del _L0_gnn_all

    def _L1_gnn_setup():
        import jax, jax.numpy as jnp
        import numpy as np
        N_NODES = 100000
        N_EDGES = 25000
        D = 64
        N_LAYERS = 3

        def _sage_conv(x, src, dst, Wl, Wr, b, n_nodes):
            msgs = x[src]
            summed = jax.ops.segment_sum(msgs, dst, num_segments=n_nodes)
            cnt = jax.ops.segment_sum(jnp.ones(src.shape[0], x.dtype), dst, num_segments=n_nodes)
            agg = summed / jnp.maximum(cnt, 1.0)[:, None]
            return agg @ Wl + x @ Wr + b
        key = jax.random.key(seed)
        k1, k2, k3, k4 = jax.random.split(key, 4)
        x = jax.random.normal(k1, (N_NODES, D), dtype=jnp.float32)
        edge_index = jax.random.randint(k2, (2, N_EDGES), 0, N_NODES, dtype=jnp.int64)
        scale = 1.0 / np.sqrt(D)
        Wl = jax.random.normal(k3, (N_LAYERS, D, D), dtype=jnp.float32) * scale
        Wr = jax.random.normal(k4, (N_LAYERS, D, D), dtype=jnp.float32) * scale
        b = jnp.zeros((N_LAYERS, D), dtype=jnp.float32)
        return {'x': x, 'edge_index': edge_index, 'Wl': Wl, 'Wr': Wr, 'b': b}
    _L1_gnn_all = _L1_gnn_setup()
    _L1_gnn_in = {k: v for k, v in _L1_gnn_all.items() if k in ('Wl', 'Wr', 'b')}
    del _L1_gnn_all

    def _L2_gnn_setup():
        import jax, jax.numpy as jnp
        import numpy as np
        N_NODES = 100000
        N_EDGES = 25000
        D_IN = 64
        D_OUT = 64
        key = jax.random.key(seed)
        k1, k2, k3, k4, k5 = jax.random.split(key, 5)
        feat = jax.random.normal(k1, (N_NODES, D_IN), dtype=jnp.float32)
        weight1 = jax.random.normal(k2, (D_IN, D_OUT), dtype=jnp.float32) * (1.0 / np.sqrt(D_IN))
        weight2 = jax.random.normal(k3, (D_IN, D_OUT), dtype=jnp.float32) * (1.0 / np.sqrt(D_IN))
        src = jax.random.randint(k4, (N_EDGES,), 0, N_NODES, dtype=jnp.int32)
        dst = jax.random.randint(k5, (N_EDGES,), 0, N_NODES, dtype=jnp.int32)
        return {'feat': feat, 'weight1': weight1, 'weight2': weight2, 'src': src, 'dst': dst}
    _L2_gnn_all = _L2_gnn_setup()
    _L2_gnn_in = {k: v for k, v in _L2_gnn_all.items() if k in ('weight1', 'weight2')}
    del _L2_gnn_all

    def _L3_gnn_setup():
        import jax, jax.numpy as jnp
        import numpy as np
        N, E_RAND, F_IN = (50000, 12500, 64)
        H1, C1 = (4, 32)
        H2, C2 = (1, 64)
        NEG_SLOPE = 0.2

        def gatv2(x, edge_index, Wl, bl, Wr, br, att, bias, H, C, concat):
            n = x.shape[0]
            src, dst = (edge_index[0], edge_index[1])
            xl = (x @ Wl.T + bl).reshape(n, H, C)
            xr = (x @ Wr.T + br).reshape(n, H, C)
            s = jax.nn.leaky_relu(xl[src] + xr[dst], NEG_SLOPE)
            e = jnp.einsum('ehc,hc->eh', s, att)
            m = jax.ops.segment_max(e, dst, num_segments=n)
            p = jnp.exp(e - m[dst])
            z = jax.ops.segment_sum(p, dst, num_segments=n)
            alpha = p / (z[dst] + 1e-16)
            out = jax.ops.segment_sum(xl[src] * alpha[:, :, None], dst, num_segments=n)
            out = out.reshape(n, H * C) if concat else out.mean(axis=1)
            return out + bias
        key = jax.random.key(seed)
        ks = jax.random.split(key, 16)
        er = jax.random.randint(ks[0], (2, E_RAND), 0, N)
        sl = jnp.tile(jnp.arange(N, dtype=er.dtype)[None, :], (2, 1))
        edge_index = jnp.concatenate([er, sl], axis=1)
        x = jax.random.normal(ks[1], (N, F_IN), dtype=jnp.float32)

        def lin(k, fan_out, fan_in):
            s = 1.0 / np.sqrt(fan_in)
            return jax.random.normal(k, (fan_out, fan_in), dtype=jnp.float32) * s
        inp = {'x': x, 'edge_index': edge_index, 'Wl1': lin(ks[2], H1 * C1, F_IN), 'bl1': jnp.zeros((H1 * C1,), jnp.float32), 'Wr1': lin(ks[3], H1 * C1, F_IN), 'br1': jnp.zeros((H1 * C1,), jnp.float32), 'att1': jax.random.normal(ks[4], (H1, C1), dtype=jnp.float32) * (1.0 / np.sqrt(C1)), 'bias1': jnp.zeros((H1 * C1,), jnp.float32), 'Wl2': lin(ks[5], H2 * C2, H1 * C1), 'bl2': jnp.zeros((H2 * C2,), jnp.float32), 'Wr2': lin(ks[6], H2 * C2, H1 * C1), 'br2': jnp.zeros((H2 * C2,), jnp.float32), 'att2': jax.random.normal(ks[7], (H2, C2), dtype=jnp.float32) * (1.0 / np.sqrt(C2)), 'bias2': jnp.zeros((C2,), jnp.float32)}
        return inp
    _L3_gnn_all = _L3_gnn_setup()
    _L3_gnn_in = {k: v for k, v in _L3_gnn_all.items() if k in ('Wl1', 'bl1', 'Wr1', 'br1', 'att1', 'bias1', 'Wl2', 'bl2', 'Wr2', 'br2', 'att2', 'bias2')}
    del _L3_gnn_all
    return {'x': x, 'src': src, 'dst': dst, 'edge_type_16': edge_type_16, 'L0_gnn_weight': _L0_gnn_in['weight'], 'L1_gnn_Wl': _L1_gnn_in['Wl'], 'L1_gnn_Wr': _L1_gnn_in['Wr'], 'L1_gnn_b': _L1_gnn_in['b'], 'L2_gnn_weight1': _L2_gnn_in['weight1'], 'L2_gnn_weight2': _L2_gnn_in['weight2'], 'L3_gnn_Wl1': _L3_gnn_in['Wl1'], 'L3_gnn_bl1': _L3_gnn_in['bl1'], 'L3_gnn_Wr1': _L3_gnn_in['Wr1'], 'L3_gnn_br1': _L3_gnn_in['br1'], 'L3_gnn_att1': _L3_gnn_in['att1'], 'L3_gnn_bias1': _L3_gnn_in['bias1'], 'L3_gnn_Wl2': _L3_gnn_in['Wl2'], 'L3_gnn_bl2': _L3_gnn_in['bl2'], 'L3_gnn_Wr2': _L3_gnn_in['Wr2'], 'L3_gnn_br2': _L3_gnn_in['br2'], 'L3_gnn_att2': _L3_gnn_in['att2'], 'L3_gnn_bias2': _L3_gnn_in['bias2']}

def reference(x, src, dst, edge_type_16, L0_gnn_weight, L1_gnn_Wl, L1_gnn_Wr, L1_gnn_b, L2_gnn_weight1, L2_gnn_weight2, L3_gnn_Wl1, L3_gnn_bl1, L3_gnn_Wr1, L3_gnn_br1, L3_gnn_att1, L3_gnn_bias1, L3_gnn_Wl2, L3_gnn_bl2, L3_gnn_Wr2, L3_gnn_br2, L3_gnn_att2, L3_gnn_bias2):
    import jax
    import jax.numpy as jnp

    def _L0_gnn_ref(feat, weight, src, dst, etypes):
        import jax, jax.numpy as jnp
        import numpy as np
        N_NODES = 100000
        N_EDGES = 15625
        D_IN = 64
        D_OUT = 64
        N_RELS = 16
        h = feat[src]
        n_rels = weight.shape[0]
        e, d_out = (h.shape[0], weight.shape[2])

        def step(m, rw):
            r, w_r = rw
            mask = jnp.where(etypes == r, 1.0, 0.0).astype(h.dtype)
            m = m + mask[:, None] * (h @ w_r)
            return (m, None)
        m0 = jnp.zeros((e, d_out), dtype=h.dtype)
        m, _ = jax.lax.scan(step, m0, (jnp.arange(n_rels), weight))
        out = jax.ops.segment_sum(m, dst, num_segments=feat.shape[0])
        return out

    def _L1_gnn_ref(x, edge_index, Wl, Wr, b):
        import jax, jax.numpy as jnp
        import numpy as np
        N_NODES = 100000
        N_EDGES = 25000
        D = 64
        N_LAYERS = 3

        def _sage_conv(x, src, dst, Wl, Wr, b, n_nodes):
            msgs = x[src]
            summed = jax.ops.segment_sum(msgs, dst, num_segments=n_nodes)
            cnt = jax.ops.segment_sum(jnp.ones(src.shape[0], x.dtype), dst, num_segments=n_nodes)
            agg = summed / jnp.maximum(cnt, 1.0)[:, None]
            return agg @ Wl + x @ Wr + b
        src, dst = (edge_index[0], edge_index[1])
        n = x.shape[0]
        h = x
        for i in range(N_LAYERS - 1):
            h = _sage_conv(h, src, dst, Wl[i], Wr[i], b[i], n)
            h = jax.nn.relu(h)
        h = _sage_conv(h, src, dst, Wl[-1], Wr[-1], b[-1], n)
        return h

    def _L2_gnn_ref(feat, weight1, weight2, src, dst):
        import jax, jax.numpy as jnp
        import numpy as np
        N_NODES = 100000
        N_EDGES = 25000
        D_IN = 64
        D_OUT = 64
        N = feat.shape[0]
        ones_e = jnp.ones(src.shape[0], dtype=feat.dtype)
        out_deg = jnp.clip(jax.ops.segment_sum(ones_e, src, num_segments=N), 1.0)
        feat_n = feat * jax.lax.rsqrt(out_deg)[:, None]
        h_src = feat_n[src]
        copy_sum = jax.ops.segment_sum(h_src, dst, num_segments=N)
        inner_sum = jax.ops.segment_sum(h_src * feat_n[dst], dst, num_segments=N)
        rst = copy_sum @ weight1 + inner_sum @ weight2
        in_deg = jnp.clip(jax.ops.segment_sum(ones_e, dst, num_segments=N), 1.0)
        rst = rst * jax.lax.rsqrt(in_deg)[:, None]
        return rst

    def _L3_gnn_ref(x, edge_index, Wl1, bl1, Wr1, br1, att1, bias1, Wl2, bl2, Wr2, br2, att2, bias2):
        import jax, jax.numpy as jnp
        import numpy as np
        N, E_RAND, F_IN = (50000, 12500, 64)
        H1, C1 = (4, 32)
        H2, C2 = (1, 64)
        NEG_SLOPE = 0.2

        def gatv2(x, edge_index, Wl, bl, Wr, br, att, bias, H, C, concat):
            n = x.shape[0]
            src, dst = (edge_index[0], edge_index[1])
            xl = (x @ Wl.T + bl).reshape(n, H, C)
            xr = (x @ Wr.T + br).reshape(n, H, C)
            s = jax.nn.leaky_relu(xl[src] + xr[dst], NEG_SLOPE)
            e = jnp.einsum('ehc,hc->eh', s, att)
            m = jax.ops.segment_max(e, dst, num_segments=n)
            p = jnp.exp(e - m[dst])
            z = jax.ops.segment_sum(p, dst, num_segments=n)
            alpha = p / (z[dst] + 1e-16)
            out = jax.ops.segment_sum(xl[src] * alpha[:, :, None], dst, num_segments=n)
            out = out.reshape(n, H * C) if concat else out.mean(axis=1)
            return out + bias
        h = gatv2(x, edge_index, Wl1, bl1, Wr1, br1, att1, bias1, H1, C1, True)
        h = jax.nn.elu(h)
        out = gatv2(h, edge_index, Wl2, bl2, Wr2, br2, att2, bias2, H2, C2, False)
        return out
    edge_index = jnp.stack([src, dst])
    h = jnp.maximum(_layernorm(x, axis=-1), 0.0)
    x = x + _L0_gnn_ref(h, L0_gnn_weight, src, dst, edge_type_16)
    h = jnp.maximum(_layernorm(x, axis=-1), 0.0)
    x = x + _L1_gnn_ref(h, edge_index, L1_gnn_Wl, L1_gnn_Wr, L1_gnn_b)
    h = jnp.maximum(_layernorm(x, axis=-1), 0.0)
    x = x + _L2_gnn_ref(h, L2_gnn_weight1, L2_gnn_weight2, src, dst)
    h = jnp.maximum(_layernorm(x, axis=-1), 0.0)
    x = x + _L3_gnn_ref(h, edge_index, L3_gnn_Wl1, L3_gnn_bl1, L3_gnn_Wr1, L3_gnn_br1, L3_gnn_att1, L3_gnn_bias1, L3_gnn_Wl2, L3_gnn_bl2, L3_gnn_Wr2, L3_gnn_br2, L3_gnn_att2, L3_gnn_bias2)
    return x

_drawn_inputs = setup_inputs


def setup_inputs(seed=0):
    import zlib

    import numpy as np

    out = dict(_drawn_inputs(seed))
    spreads = {'L1_gnn_b': (0.0, 0.1),
     'L3_gnn_bl1': (0.0, 0.314),
     'L3_gnn_br1': (0.0, 0.8),
     'L3_gnn_bias1': (0.0, 0.1),
     'L3_gnn_bl2': (0.0, 0.1),
     'L3_gnn_br2': (0.0, 0.8),
     'L3_gnn_bias2': (0.0, 0.1)}
    factors = {'L3_gnn_Wr1': 8.0, 'L3_gnn_att1': 4.749, 'L3_gnn_Wr2': 8.0, 'L3_gnn_att2': 5.276}
    for name, (base, spread) in spreads.items():
        noise = np.random.default_rng([zlib.crc32(name.encode()), seed]).standard_normal(out[name].shape)
        drawn = base * np.exp(spread * noise) if base else spread * noise
        out[name] = jnp.asarray(drawn.astype(out[name].dtype))
    for name, factor in factors.items():
        out[name] = (out[name] * factor).astype(out[name].dtype)
    return out
```

```python
from contextlib import ExitStack

import numpy as np

import concourse.bass as bass
from concourse import mybir

ALU = mybir.AluOpType
ACT = mybir.ActivationFunctionType
F32 = mybir.dt.float32
F16 = mybir.dt.float16
I32 = mybir.dt.int32
AX_X = mybir.AxisListType.X

P = 128
N = 100000
E = 50000
D = 64
D2 = 2 * D
C = 28
CHUNKS = 14
TURNS = CHUNKS // 2
TILES = C * CHUNKS
ROWS = P * TILES
G4 = 4
GROUPS = C // G4
PC = 14
PCHUNKS = TILES // PC
NP_ = 125
NT = N // NP_
NC = 20
NCHUNKS = NT // NC
NGROUPS = NC // G4
RELS = 16
HEADS = 4
HI = (N >> 8) + 1
LOB = 2
PAD = 131071
FAR = 131072.0
BIG = 1.0e30
EPS = 1.0e-5
WEIGHT_LOADS = 22
HSLOT = 3 * (HI + 1) + 2 * 256
HCOLS = 4
HTURNS = TILES // (2 * HCOLS)
(DF, DL, JP, JN, WH, PEN_P, PEN_N, CAP_P, CAP_N, FT_ROW, FT_HAS, FT_OUT, INV_FT, RSIN_FT, RSDST_FT,
 MISS, SCR, CNT_C) = range(18)
IX_FT, IX_FTG, IX_LASTQ, IX_LAST, IX_OUT, SCR_I, SCR_J, NEG = range(8)


class Chain:

    def __init__(self, eng, sem):
        self.eng, self.sem, self.n = eng, sem, 0

    def reset(self):
        if self.n:
            self.eng.wait_ge(self.sem, 1)
        self.eng.sem_clear(self.sem)
        self.n = 0

    def __call__(self, ins):
        self.n += 1
        ins.then_inc(self.sem, 1)
        self.eng.wait_ge(self.sem, self.n)


def build_program(nc, x, src, dst, etype, w0, wl, wr, wb, w1, w2, gwl1, gbl1, gwr1, gbr1, gatt1, gbias1,
                  gwl2, gbl2, gwr2, gbr2, gatt2, gbias2, out):
    with ExitStack() as ctx:
        def sb(name, shape, dt=F32):
            return ctx.enter_context(nc.sbuf_tensor(name, shape, dt))

        def dram(name, shape, dt=F32):
            return nc.dram_tensor(name, shape, dt, kind="Internal").ap()

        def rows(name, width=D):
            return dram(name, [P, TILES * width])

        def by_row(t, width=D):
            return t.rearrange("p (t f) -> (p t) f", f=width)

        xsrc, xdst = rows("x_of_src"), rows("x_of_dst")
        lone = [rows(f"lone_state{k}") for k in range(4)]
        table = [rows(f"table{k}") for k in range(5)]
        total = [rows(f"total{k}") for k in range(5)]
        total_g1, total_g2 = rows("total_gat1", D2), rows("total_gat2")
        resid = [rows(f"resid{k}") for k in range(3)]
        xl1 = rows("xl1_of_src", D2)
        table_l2, table_r2 = rows("table_xl2"), rows("table_xr2")
        xl2 = rows("xl2_of_src")
        lone_xl2 = dram("lone_xl2", [P, C * D])
        dst_line = dram("dst_line", [ROWS + 2, 1], I32)
        node_info = dram("node_info", [P * LOB * HI, 2])

        def edges(name, dt=F32):
            return sb(name, [P, TILES], dt)

        same, tail, rest = edges("same"), edges("tail"), edges("rest")
        first_seg, last_seg, first_tail = edges("first_seg"), edges("last_seg"), edges("first_tail")
        inv_in, rs_in, rs_src, rs_dst = edges("inv_in"), edges("rs_in"), edges("rs_src"), edges("rs_dst")
        etf = edges("etf")
        tmp = edges("tmp")
        srci, dsti = edges("srci", I32), edges("dsti", I32)
        srcq, dstq = edges("srcq", I32), edges("dstq", I32)
        EE = sb("EE", [P, 3 * HEADS, TILES])
        Ea, Eb, Ec = EE[:, 0:HEADS, :], EE[:, HEADS:2 * HEADS, :], EE[:, 2 * HEADS:, :]
        G = sb("G", [P, 2, C * D])
        XB = sb("XB", [P, 2, C * D])
        HH = sb("HH", [P, 2, C * D2])
        R = sb("R", [P, 2, C * D2])
        O = sb("O", [P, 2, C * D2])
        PG = sb("PG", [P, 2, PC * D])
        AT = sb("AT", [P, 2, 512])
        SX = sb("SX", [P, 2, 1024])
        XC = sb("XC", [P, C * D])
        SQ = sb("SQ", [P, C * D])
        IW = sb("IW", [P, 2, C], I32)
        st = sb("st", [P, 4, C])
        fw = sb("fw", [P, 2, 6, HCOLS])
        info = XC[:, 0:LOB * HI * 2].rearrange("p (l h c) -> p l h c", l=LOB, c=2)
        ident = sb("ident", [P, P])
        iota_h = sb("iota_h", [P, HI + 1], F16)
        iota_r = sb("iota_r", [P, RELS])
        ones = sb("ones", [1, P])
        zeroh = sb("zeroh", [P, 512], F16)
        epsc = sb("epsc", [P, 1])
        W0 = sb("W0", [P, RELS // 2, D])
        WD = sb("WD", [P, 3, D])
        WS = sb("WS", [P, 3, D2])
        W12 = sb("W12", [P, D])
        WG1 = sb("WG1", [P, 2 * D2])
        WG2 = sb("WG2", [P, D2])
        BS = sb("BS", [1, 3, D2])
        BG1 = sb("BG1", [1, 2 * D2])
        BG2 = sb("BG2", [1, D2])
        attb1 = sb("attb1", [P, D2])
        attb2 = sb("attb2", [P, D])
        bias1c = sb("bias1c", [P, 1])
        bias2b = sb("bias2b", [P, D])
        CARRY = sb("CARRY", [P, P])
        cols = sb("cols", [P, 32])
        colsi = sb("colsi", [P, 8], I32)
        rowz = sb("rowz", [HEADS, 8, P])
        tz = sb("tz", [P, 8, HEADS])
        VB = sb("VB", [P, D])

        PS = ctx.enter_context(nc.psum_tensor("PS", [P, 8, 512], F32))

        def sem(name):
            return ctx.enter_context(nc.semaphore(name))

        bar = sem("phase_ended")
        chv, cha, chp = sem("dve_step"), sem("act_step"), sem("pool_step")
        s_fill, s_const = sem("fills_made"), sem("constants_made")
        s_in, s_w = sem("indices_loaded"), sem("weights_loaded")
        s_line, s_shift = sem("dst_line_stored"), sem("shifted_dst_loaded")
        s_keys = sem("index_columns_made")
        s_cols = sem("partition_columns_made")
        s_trans = sem("setup_products_made")
        s_hot, s_binned, s_bins, s_info = sem("one_hots_made"), sem("one_hots_used"), sem("bins_made"), sem("node_info_stored")
        s_pg, s_pst, s_infog = [sem("x_rows_gathered0"), sem("x_rows_gathered1")], [sem("x_rows_stored0"), sem("x_rows_stored1")], sem("info_gathered")
        s_infoc = sem("info_copied")
        s_xc, s_sq, s_var, s_std = sem("ln_centred"), sem("ln_squared"), sem("ln_variance"), sem("ln_deviation")

        s_ld, s_st = [sem("loaded0"), sem("loaded1")], [sem("stored0"), sem("stored1")]
        s_turned, s_copied = sem("groups_transposed"), sem("transposed_copied")
        s_mult, s_out = sem("groups_multiplied"), sem("products_copied")
        s_ready, s_done = sem("chunk_ready"), sem("chunk_done")
        s_carry = sem("carry_multiplied")
        s_ldg = [sem("defaults_loaded0"), sem("defaults_loaded1")]
        s_g = [sem("gathered0"), sem("gathered1")]
        s_scan = sem("chunk_scanned")
        s_patch, s_patched = sem("patch_rows_gathered"), sem("patch_rows_scattered")
        s_prep, s_lone = sem("prep_step"), sem("lone_xl2_stored")
        s_scored, s_exp, s_elu = sem("groups_scored"), sem("exponentials_made"), sem("elu_made")
        s_sm = sem("softmax_step")
        s_last = sem("last_tails_known")
        s_scan2 = sem("dst_rows_spread")
        SM_STEPS = 17
        s_sc = [sem("output_rows_scattered0"), sem("output_rows_scattered1")]
        s_mask, s_mturned = sem("masked_rows_made"), sem("masked_rows_transposed")
        s_mcopied, s_mmult, s_mout = sem("masked_copied"), sem("messages_multiplied"), sem("messages_copied")

        counts, before = {}, {}

        def plan(phase, **adds):
            for name, n in adds.items():
                before[phase, name] = counts.get(name, 0)
                counts[name] = counts.get(name, 0) + n

        plan("source", ld=TURNS * 16, st=5 * TURNS * 16, ln=2 * CHUNKS, group=3 * GROUPS * CHUNKS, ready=CHUNKS, done=CHUNKS, carry=1)
        plan("dest", ld=2 * TURNS * 16, st=2 * TURNS * 16, ln=CHUNKS, done=CHUNKS)
        plan("nodes", ld=NCHUNKS // 2 * 16, st=NCHUNKS // 2 * 16, ln=NCHUNKS, group=3 * NGROUPS * NCHUNKS, ready=NCHUNKS, done=NCHUNKS)
        plan("prep", patch=16, carry=1)
        LAYERS = [f"layer{k}" for k in range(4)]
        for k, layer in enumerate(LAYERS):
            normed = k >= 2
            plan(layer, ldg=TURNS * 16, ld=(1 + normed) * TURNS * 16, st=(3 if normed else 2) * TURNS * 16, gath=TURNS * 16 * C,
                 scan=CHUNKS, ready=CHUNKS + 1, group=GROUPS * CHUNKS + 1, done=(CHUNKS + 1) * normed, ln=normed * (CHUNKS + 1), carry=1,
                 patch=(2 + normed) * 16, patched=(1 + normed) * 16)
        plan("att1", ldg=TURNS * 16, ld=TURNS * 16, st=TURNS * 16, gath=TURNS * 16 * C, ready=CHUNKS, group=GROUPS * CHUNKS, patch=16)
        plan("sum1", ld=TURNS * 16, st=3 * TURNS * 16, scan=CHUNKS, ready=CHUNKS + 1, group=GROUPS * CHUNKS + 1, carry=1,
             patch=16, patched=32)
        plan("att2", ldg=TURNS * 16, ld=TURNS * 16, st=TURNS * 16, gath=TURNS * 16 * C, done=CHUNKS, patch=16)
        plan("sum2", ld=2 * TURNS * 16, st=TURNS * 16, scan=CHUNKS, ready=CHUNKS, carry=1, patch=32, patched=16)
        BAR = {name: n for n, name in enumerate(["setup", "bins", "source", "dest", "nodes", "prep"])}
        for name in LAYERS:
            BAR[name] = len(BAR)
            BAR[name + " patch"] = len(BAR)
        for name in ("att1", "soft1", "sum1", "sum1 patch", "att2", "soft2", "sum2", "sum2 patch"):
            BAR[name] = len(BAR)
        AHEAD = 2

        def chunk(t, c, width):
            return t[:, bass.ds(c * width, width)]

        def over(ap, n):
            return ap.unsqueeze(2).broadcast_to([ap.shape[0], ap.shape[1], n])

        def cut(ap, n=D):
            return ap.rearrange("p (m n) -> p m n", n=n)

        def paired(eng, turns, body, start=0):
            with eng.Fori(start, turns) as it:
                for b in range(2):
                    body(2 * it + b, it, b)

        class Barrier:

            def __init__(self, eng):
                self.eng, self.n = eng, 0

            def __call__(self):
                self.n += 1
                self.eng.drain().then_inc(bar, 1)
                self.eng.wait_ge(bar, 4 * self.n)

        def phases_over(eng, n):
            eng.wait_ge(bar, 4 * n)

        block = ctx.enter_context(nc.Block())

        @block.sync
        def _(sp):
            barrier = Barrier(sp)
            FULL = P - 1
            REST = E - FULL * TILES
            sp.wait_ge(s_fill, 5)
            for to, of in ((dsti, dst), (srci, src), (tmp[:].bitcast(I32), etype)):
                sp.dma_start(to[0:FULL, :], of[0:FULL * TILES].rearrange("(p t) -> p t", t=TILES)).then_inc(s_in, 16)
                sp.dma_start(to[FULL:P, 0:REST], of[FULL * TILES:E].rearrange("(p t) -> p t", p=1)).then_inc(s_in, 16)
            loads = [(W0[r * D:(r + 1) * D], w0.rearrange("(j r) k o -> r k j o", r=2)[r]) for r in range(2)]
            loads += [(WD[0:D], wl.rearrange("l k o -> k l o")), (WD[D:P], wr.rearrange("l k o -> k l o"))]
            loads += [(WS[r * D:(r + 1) * D, :, r * D:(r + 1) * D], wr.rearrange("l k o -> k l o")) for r in range(2)]
            loads += [(W12[0:D], w1), (W12[D:P], w2)]
            loads += [(SQ[:, 0:D], gwl1), (SQ[:, D:D2], gwr1), (SQ[0:D, D2:2 * D2], gwl2), (SQ[D:P, D2:2 * D2], gwr2)]
            loads += [(BS[:, :, r * D:(r + 1) * D], wb.unsqueeze(0)) for r in range(2)]
            loads += [(BG1[:, D2:], gbl1.unsqueeze(0)), (BG1[:, 0:D2], gbr1.unsqueeze(0))]
            loads += [(BG2[:, 0:D], gbl2.unsqueeze(0)), (BG2[:, D:], gbr2.unsqueeze(0))]
            loads += [(attb1[:], gatt1.rearrange("h c -> (h c)").partition_broadcast(P)),
                      (attb2[:], gatt2.rearrange("h c -> (h c)").partition_broadcast(P)),
                      (bias2b[:], gbias2.partition_broadcast(P)), (bias1c[:], gbias1.unsqueeze(1))]
            assert len(loads) == WEIGHT_LOADS
            for to, of in loads:
                sp.dma_start(to, of).then_inc(s_w, 16)
            sp.wait_ge(s_in, 16 * 6)
            sp.dma_start(dst_line[1:ROWS + 1, :].rearrange("(p t) o -> p (t o)", t=TILES), dsti[:]).then_inc(s_line, 16)
            sp.dma_start(dst_line[0:1, :], colsi[0:1, NEG:NEG + 1]).then_inc(s_line, 16)
            sp.dma_start(dst_line[ROWS + 1:ROWS + 2, :], colsi[0:1, NEG:NEG + 1]).then_inc(s_line, 16)
            sp.wait_ge(s_line, 48)
            for to, at in ((Ea[:, 0, :], 0), (Ea[:, 1, :], 2)):
                sp.dma_start(to.bitcast(I32), dst_line[at:at + ROWS, :].rearrange("(p t) o -> p (t o)", t=TILES)
                             ).then_inc(s_shift, 16)
            barrier()
            sp.wait_ge(s_bins, 1)
            sp.dma_start(node_info.rearrange("(p r) c -> p (r c)", p=P), info.rearrange("p l h c -> p (l h c)")
                         ).then_inc(s_info, 16)
            sp.wait_ge(s_info, 16)
            barrier()

            def streams(phase, chunks, loads, stores, begin=None):
                def load(i, it, b):
                    if begin:
                        begin(i, it, b)
                    for to, of in loads(i, b):
                        sp.dma_start(to, of).then_inc(s_ld[b], 16)

                def store(i, it, b):
                    sp.wait_ge(s_done, before[phase, "done"] + 1 + i)
                    for to, of in stores(i, b):
                        sp.dma_start(to, of).then_inc(s_st[b], 16)
                    sp.wait_ge(s_st[b], before[phase, "st"] + 16 * len(stores(0, 0)) * (it + 1))

                for b in range(2):
                    load(b, 0, b)

                def turn(i, it, b):
                    store(i, it, b)
                    load(i + 2, it + 1, b)

                paired(sp, chunks // 2 - 1, turn)
                for b in range(2):
                    store(chunks - 2 + b, chunks // 2 - 1, b)

            def x_rows_there(which):
                def wait(i, it, b):
                    for k in range(2):
                        sp.wait_ge(s_pst[k], 16 * (which * (PCHUNKS // 2) + 1 + i))
                return wait

            CD = C * D
            streams("source", CHUNKS, lambda i, b: [(XB[:, b, :], chunk(xsrc, i, CD))],
                    lambda i, b: [(chunk(lone[0], i, CD), G[:, b, :]), (chunk(lone[1], i, CD), HH[:, b, 0:CD]),
                                  (chunk(lone[2], i, CD), HH[:, b, CD:]), (chunk(lone[3], i, CD), O[:, b, 0:CD]),
                                  (chunk(total[0], i, CD), R[:, b, CD:])], x_rows_there(0))
            barrier()
            streams("dest", CHUNKS, lambda i, b: [(XB[:, b, :], chunk(xdst, i, CD)), (R[:, b, 0:CD], chunk(total[0], i, CD))],
                    lambda i, b: [(chunk(resid[0], i, CD), XB[:, b, :]), (chunk(table[0], i, CD), G[:, b, :])], x_rows_there(1))
            barrier()
            x_nodes, out_nodes = (t.rearrange("(p t) f -> p (t f)", p=NP_) for t in (x, out))
            streams("nodes", NCHUNKS, lambda i, b: [(XB[0:NP_, b, 0:NC * D], chunk(x_nodes, i, NC * D))],
                    lambda i, b: [(chunk(out_nodes, i, NC * D), XB[0:NP_, b, 0:NC * D])])
            barrier()
            sp.wait_ge(s_prep, 4)
            sp.dma_start(lone_xl2, XC[:]).then_inc(s_lone, 16)
            sp.wait_ge(s_lone, 16)
            barrier()

            def layer_streams(phase, early, late, stores, early_free, finished, c_of=lambda i: i):
                def load_early(i, it, b):
                    for to, of in early(c_of(i), b):
                        sp.dma_start(to, of).then_inc(s_ldg[b], 16)

                def load_late(i, it, b):
                    for to, of in late(c_of(i), b):
                        sp.dma_start(to, of).then_inc(s_ld[b], 16)

                def store(i, it, b):
                    finished(i, b)
                    for to, of in stores(c_of(i), b):
                        sp.dma_start(to, of).then_inc(s_st[b], 16)
                    sp.wait_ge(s_st[b], before[phase, "st"] + 16 * len(stores(0, 0)) * (it + 1))

                for b in range(2):
                    load_early(b, 0, b)
                    load_late(b, 0, b)

                def turn(i, it, b):
                    if early_free:
                        early_free(i)
                        load_early(i + 2, it + 1, b)
                    store(i, it, b)
                    if not early_free:
                        load_early(i + 2, it + 1, b)
                    load_late(i + 2, it + 1, b)

                paired(sp, TURNS - 1, turn)
                for b in range(2):
                    store(CHUNKS - 2 + b, TURNS - 1, b)

            def products_out(phase):
                def wait(i, b):
                    sp.wait_ge(s_out, before[phase, "group"] + AHEAD + GROUPS * (i + 1))
                return wait

            def chunk_done(phase):
                def wait(i, b):
                    sp.wait_ge(s_done, before[phase, "done"] + 1 + i)
                return wait

            def patched(phase, n):
                sp.wait_ge(s_patched, before[phase, "patched"] + 16 * n)

            for k, layer in enumerate(LAYERS):
                normed = k >= 2
                right = lambda b: cut(HH[:, b, :], D2)[:, :, D:]
                layer_streams(
                    layer, lambda c, b: [(G[:, b, :], chunk(lone[k], c, CD))],
                    lambda c, b: [(right(b), cut(chunk(table[k], c, CD)))] + [(XB[:, b, :], chunk(resid[k - 2], c, CD))] * normed,
                    lambda c, b: [(chunk(total[k + 1], c, CD), R[:, b, 0:CD]), (chunk(table[k + 1], c, CD), O[:, b, 0:CD])]
                    + [(chunk(resid[k - 1], c, CD), XB[:, b, :])] * normed,
                    lambda i: sp.wait_ge(s_scan, before[layer, "scan"] + 1 + i),
                    chunk_done(layer) if normed else products_out(layer))
                barrier()
                patched(layer, 1 + normed)
                barrier()
            layer_streams(
                "att1", lambda c, b: [(cut(HH[:, b, :], D2)[:, :, 0:D], cut(chunk(lone[3], c, CD)))],
                lambda c, b: [(XB[:, b, :], chunk(table[4], c, CD))],
                lambda c, b: [(chunk(xl1, c, 2 * CD), O[:, b, :])],
                lambda i: sp.wait_ge(s_turned, before["att1", "group"] + GROUPS * (i + 1)),
                products_out("att1"), lambda i: (CHUNKS - 1) - i if isinstance(i, int) else i * (-1) + (CHUNKS - 1))
            barrier()
            barrier()
            layer_streams(
                "sum1", lambda c, b: [], lambda c, b: [(HH[:, b, :], chunk(xl1, c, 2 * CD))],
                lambda c, b: [(chunk(total_g1, c, 2 * CD), R[:, b, :]), (chunk(table_l2, c, CD), O[:, b, 0:CD]),
                              (chunk(table_r2, c, CD), O[:, b, CD:])],
                None, products_out("sum1"))
            barrier()
            patched("sum1", 2)
            barrier()
            layer_streams(
                "att2", lambda c, b: [(G[:, b, :], lone_xl2)],
                lambda c, b: [(XB[:, b, :], chunk(table_r2, c, CD))],
                lambda c, b: [(chunk(xl2, c, CD), G[:, b, :])],
                None, chunk_done("att2"), lambda i: (CHUNKS - 1) - i if isinstance(i, int) else i * (-1) + (CHUNKS - 1))
            barrier()
            barrier()

            def scattered(i, b):
                sp.wait_ge(s_ready, before["sum2", "ready"] + 1 + i)
                sp.wait_ge(s_sc[b], 16 * C * ((i - b) // 2 + 1) if isinstance(i, int) else (i - b) * (8 * C) + 16 * C)

            layer_streams(
                "sum2", lambda c, b: [], lambda c, b: [(G[:, b, :], chunk(xl2, c, CD)), (XB[:, b, :], chunk(resid[2], c, CD))],
                lambda c, b: [(chunk(total_g2, c, CD), R[:, b, 0:CD])], None, scattered)
            barrier()
            patched("sum2", 1)
            barrier()

        @block.gpsimd
        def _(pool):
            step = Chain(pool, chp)
            pool.memset(dsti[:], PAD).then_inc(s_fill, 1)
            pool.memset(srci[:], PAD).then_inc(s_fill, 1)
            pool.memset(tmp[:].bitcast(I32), 0).then_inc(s_fill, 1)
            pool.memset(colsi[:], -1).then_inc(s_fill, 1)
            pool.memset(WS[:], 0.0).then_inc(s_fill, 1)
            step(pool.memset(ident[:], 0.0))
            pool.affine_select(out=ident[:], in_=ident[:], compare_op=ALU.not_equal, fill=1.0, base=0,
                               pattern=[[-1, P]], channel_multiplier=1).then_inc(s_const, 1)
            step(pool.memset(CARRY[:], 1.0))
            pool.affine_select(out=CARRY[:], in_=CARRY[:], compare_op=ALU.is_gt, fill=0.0, base=0,
                               pattern=[[1, P]], channel_multiplier=-1).then_inc(s_const, 1)
            pool.iota(XC[:, 0:HI + 1].bitcast(I32), pattern=[[1, HI + 1]], base=0, channel_multiplier=0).then_inc(s_const, 1)
            pool.iota(Ea[:, 2, :].bitcast(I32), pattern=[[1, TILES]], base=0, channel_multiplier=TILES).then_inc(s_const, 1)
            pool.memset(PG[:], 0.0).then_inc(s_const, 1)

            def gather(to, table_, idx, bound, signal):
                return pool.indirect_dma_start(to, None, table_, bass.IndirectOffsetOnAxis(ap=idx, axis=0),
                                               bounds_check=bound, oob_is_err=False).then_inc(signal, 16)

            pool.wait_ge(s_keys, 1)
            step(pool.memset(IW[:], 0))
            for which, (idx, to) in enumerate(((srci, xsrc), (dsti, xdst))):
                def turn(it, b, first):
                    step.reset()
                    if not first:
                        pool.wait_ge(s_pst[b], 16 * (it + which * (PCHUNKS // 2)))
                    step(pool.tensor_copy(IW[:, b, 0:PC], idx[:, bass.ds((2 * it + b) * PC, PC)]))
                    for j in range(PC):
                        gather(PG[:, b, j * D:(j + 1) * D], x, IW[:, b, j:j + 1], N - 1, s_pg[b])
                    pool.wait_ge(s_pg[b], 16 * PC * (it + 1 + which * (PCHUNKS // 2)))
                    pool.wait_ge(chp, 1)
                    pool.dma_start(chunk(to, 2 * it + b, PC * D), PG[:, b, :]).then_inc(s_pst[b], 16)
                if which == 0:
                    for b in range(2):
                        turn(0, b, True)
                with pool.Fori(1 - which, PCHUNKS // 2) as it:
                    for b in range(2):
                        turn(it, b, False)
            for b in range(2):
                pool.wait_ge(s_pst[b], 16 * PCHUNKS)
            pool.wait_ge(s_info, 16)
            for which, idx in enumerate((srcq, dstq)):
                with pool.Fori(0, CHUNKS) as i:
                    step.reset()
                    step(pool.tensor_copy(IW[:, 0, :], idx[:, bass.ds(i * C, C)]))
                    for j in range(C):
                        gather(PG[:, 0, 2 * j:2 * j + 2], node_info, IW[:, 0, j:j + 1], P * LOB * HI - 1, s_infog)
                    pool.wait_ge(s_infog, 16 * C * (i + 1 + which * CHUNKS))
                    pool.wait_ge(chp, 1)
                    step(pool.tensor_copy(EE[:, 4 * which:4 * which + 2, bass.ds(i * C, C)].rearrange("p c t -> p t c"),
                                          PG[:, 0, 0:2 * C].rearrange("p (t c) -> p t c", c=2)))
                pool.wait_ge(chp, 2)
            gather(PG[:, 0, 0:2], node_info, colsi[:, IX_LASTQ:IX_LASTQ + 1], P * LOB * HI - 1, s_patch)
            pool.drain().then_inc(s_infoc, 1)

            def after(phase):
                pool.wait_ge(bar, 4 * BAR[phase])

            def gathers(phase, table_, to):
                def turn(i, it, b):
                    step.reset()
                    pool.wait_ge(s_ldg[b], before[phase, "ldg"] + 16 * (it + 1))
                    c = i if phase in LAYERS else i * (-1) + (CHUNKS - 1)
                    step(pool.tensor_copy(IW[:, b, :], srcq[:, bass.ds(c * C, C)]))
                    for j in range(C):
                        gather(to(b, j), table_, IW[:, b, j:j + 1], ROWS - 1, s_g[b])
                paired(pool, TURNS, turn)

            def scatter(of, table_, idx, bound, signal):
                return pool.indirect_dma_start(table_, bass.IndirectOffsetOnAxis(ap=idx, axis=0), of, None,
                                               bounds_check=bound, oob_is_err=False).then_inc(signal, 16)

            at_tail, to_tail, last_tail = colsi[:, IX_FTG:IX_FTG + 1], colsi[:, IX_FT:IX_FT + 1], colsi[:, IX_LAST:IX_LAST + 1]

            for k, layer in enumerate(LAYERS):
                normed = k >= 2
                after(layer)
                gathers(layer, by_row(table[k]), lambda b, j: G[:, b, j * D:(j + 1) * D])
                after(layer + " patch")
                gather(R[:, 0, 0:D], by_row(total[k + 1]), at_tail, ROWS - 1, s_patch)
                gather(HH[:, 0, D:D2], by_row(table[k]), at_tail, ROWS - 1, s_patch)
                if normed:
                    gather(XB[:, 0, 0:D], by_row(resid[k - 2]), at_tail, ROWS - 1, s_patch)
                    pool.wait_ge(s_done, before[layer, "done"] + CHUNKS + 1)
                else:
                    pool.wait_ge(s_out, before[layer, "group"] + AHEAD + GROUPS * CHUNKS + 1)
                scatter(O[:, 0, 0:D], by_row(table[k + 1]), to_tail, ROWS - 1, s_patched)
                if normed:
                    scatter(XB[:, 0, 0:D], by_row(resid[k - 1]), to_tail, ROWS - 1, s_patched)
            after("att1")
            gather(VB[:], by_row(table[4]), last_tail, ROWS - 1, s_patch)
            gathers("att1", by_row(table[4]), lambda b, j: HH[:, b, j * D2:j * D2 + D])
            after("sum1 patch")
            gather(R[:, 0, 0:D2], by_row(total_g1, D2), at_tail, ROWS - 1, s_patch)
            pool.wait_ge(s_out, before["sum1", "group"] + AHEAD + GROUPS * CHUNKS + 1)
            scatter(O[:, 0, 0:D], by_row(table_l2), to_tail, ROWS - 1, s_patched)
            scatter(O[:, 0, C * D:C * D + D], by_row(table_r2), to_tail, ROWS - 1, s_patched)
            after("att2")
            gather(VB[:], by_row(table_r2), last_tail, ROWS - 1, s_patch)
            gathers("att2", by_row(table_l2), lambda b, j: G[:, b, j * D:(j + 1) * D])
            after("sum2")

            def output(i, it, b):
                step.reset()
                pool.wait_ge(s_ready, before["sum2", "ready"] + 1 + i)
                step(pool.tensor_copy(IW[:, b, :], dstq[:, bass.ds(i * C, C)]))
                for j in range(C):
                    scatter(O[:, b, j * D:(j + 1) * D], out, IW[:, b, j:j + 1], N - 1, s_sc[b])

            paired(pool, TURNS, output)
            after("sum2 patch")
            gather(R[:, 0, 0:D], by_row(total_g2), at_tail, ROWS - 1, s_patch)
            gather(XB[:, 0, 0:D], by_row(resid[2]), at_tail, ROWS - 1, s_patch)
            pool.wait_ge(s_sm, SM_STEPS)
            scatter(O[:, 0, 0:D], out, colsi[:, IX_OUT:IX_OUT + 1], N - 1, s_patched)
            pool.wait_ge(s_patched, counts["patched"])

        @block.vector
        def _(dve):
            step = Chain(dve, chv)
            barrier = Barrier(dve)
            cast, tt, ts = dve.tensor_copy, dve.tensor_tensor, dve.tensor_scalar

            def col(k):
                return cols[:, k:k + 1]

            def coli(k):
                return colsi[:, k:k + 1]

            step(dve.memset(zeroh[:], 0.0))
            step(dve.memset(ones[:], 1.0))
            step(dve.memset(epsc[:], EPS))
            step(dve.memset(HH[:], 0.0))
            step(dve.memset(R[:], 0.0))
            dve.wait_ge(s_const, 5)
            step(cast(iota_h[:], XC[:, 0:HI + 1].bitcast(I32)))
            step(cast(iota_r[:], XC[:, 0:RELS].bitcast(I32)))
            dve.wait_ge(s_in, 16 * 6)
            step(cast(etf[:], tmp[:].bitcast(I32)))
            scr_i, scr_f = O[:, 0, 0:TILES].bitcast(I32), O[:, 0, TILES:2 * TILES]
            acc_f = O[:, 0, 2 * TILES:3 * TILES]
            fields = {}
            for k, (key, q) in enumerate(((srci, srcq), (dsti, dstq))):
                hi_f, lo_f = EE[:, 3 + 2 * k, :], EE[:, 4 + 2 * k, :]
                fields[k] = (hi_f, lo_f)
                step(ts(scr_i, key[:], 8, None, ALU.logical_shift_right))
                step(cast(hi_f, scr_i))
                step(ts(scr_i, key[:], 255, None, ALU.bitwise_and))
                step(cast(lo_f, scr_i))
                step(ts(scr_i, key[:], 127, None, ALU.bitwise_and))
                step(cast(scr_f, scr_i))
                step(dve.scalar_tensor_tensor(out=acc_f, in0=scr_f, scalar=float(LOB * HI), in1=hi_f, op0=ALU.mult, op1=ALU.add))
                step(ts(scr_i, key[:], 7, 1, ALU.logical_shift_right, ALU.bitwise_and))
                step(cast(scr_f, scr_i))
                step(dve.scalar_tensor_tensor(out=acc_f, in0=scr_f, scalar=float(HI), in1=acc_f, op0=ALU.mult, op1=ALU.add))
                step(cast(q[:], acc_f))
            step(ts(col(SCR), acc_f[:, TILES - 1:TILES], float(P * LOB * HI - 1), None, ALU.min))
            step(cast(coli(IX_LASTQ), col(SCR)))
            dve.nop().then_inc(s_keys, 1)
            dve.wait_ge(s_shift, 32)
            dst_f, prev_f, next_f = O[:, 0, 0:TILES], O[:, 0, TILES:2 * TILES], O[:, 0, 2 * TILES:3 * TILES]
            step(cast(dst_f, dsti[:]))
            step(cast(prev_f, Ea[:, 0, :].bitcast(I32)))
            step(cast(next_f, Ea[:, 1, :].bitcast(I32)))
            step(tt(same[:], dst_f, prev_f, ALU.is_equal))
            step(tt(tail[:], dst_f, next_f, ALU.not_equal))
            step(tt(rest[:], dst_f, next_f, ALU.is_equal))
            step(cast(col(JP), same[:, 0:1]))
            step(cast(col(JN), rest[:, TILES - 1:TILES]))
            step(dve.memset(same[:, 0:1], 0.0))
            step(cast(col(DF), dst_f[:, 0:1]))
            step(cast(col(DL), dst_f[:, TILES - 1:TILES]))
            step(tt(col(WH), col(DF), col(DL), ALU.is_equal))
            step(ts(first_seg[:], dst_f, col(DF), None, ALU.is_equal))
            step(ts(last_seg[:], dst_f, col(DL), None, ALU.is_equal))
            step(tt(first_tail[:], first_seg[:], tail[:], ALU.mult))
            rowid = O[:, 0, 3 * TILES:4 * TILES]
            prod = O[:, 0, 4 * TILES:5 * TILES]
            step(cast(rowid, Ea[:, 2, :].bitcast(I32)))

            def at_first_tail(out_col, values):
                step(tt(prod, values, first_tail[:], ALU.mult))
                step(dve.tensor_reduce(out_col, prod, AX_X, ALU.add))

            at_first_tail(col(FT_ROW), rowid)
            step(dve.tensor_reduce(col(FT_HAS), first_tail[:], AX_X, ALU.add))
            at_first_tail(col(FT_OUT), dst_f)
            step(cast(coli(IX_FTG), col(FT_ROW)))
            step(ts(col(MISS), col(FT_HAS), -FAR, FAR, ALU.mult, ALU.add))
            step(tt(col(FT_ROW), col(FT_ROW), col(MISS), ALU.add))
            step(cast(coli(IX_FT), col(FT_ROW)))
            step(tt(col(FT_OUT), col(FT_OUT), col(MISS), ALU.add))
            step(cast(coli(IX_OUT), col(FT_OUT)))
            for cap, pen, join in ((CAP_P, PEN_P, JP), (CAP_N, PEN_N, JN)):
                step(ts(col(cap), col(join), BIG, -BIG, ALU.mult, ALU.add))
                step(tt(col(pen), col(join), col(WH), ALU.mult))
                step(ts(col(pen), col(pen), BIG, -BIG, ALU.mult, ALU.add))
            step(ts(prod, rowid, 1.0, None, ALU.add))
            step(tt(prod, prod, tail[:], ALU.mult))
            step(cast(scr_i, prod))
            step(ts(prev_f.bitcast(I32), scr_i, 8, None, ALU.logical_shift_right))
            step(cast(EE[:, 7, :], prev_f.bitcast(I32)))
            step(ts(prev_f.bitcast(I32), scr_i, 255, None, ALU.bitwise_and))
            step(cast(EE[:, 8, :], prev_f.bitcast(I32)))
            dve.nop().then_inc(s_cols, 1)
            dve.wait_ge(s_trans, 1)
            step(ts(prod[:, 0:P], PS[:, 0, 0:P], col(DL), None, ALU.is_equal))
            step(tt(CARRY[:], CARRY[:], prod[:, 0:P], ALU.mult))
            dve.wait_ge(s_trans, 3)
            dve.wait_ge(s_w, 16 * WEIGHT_LOADS)
            step(cast(WG1[:, 0:D2], PS[:, 1, 0:D2]))
            step(cast(WG1[0:D, D2:], PS[0:D, 1, 0:D2]))
            step(dve.memset(WG1[D:P, D2:], 0.0))
            step(cast(WG2[:], PS[:, 1, D2:2 * D2]))
            step(tt(BG1[:, 0:D2], BG1[:, 0:D2], BG1[:, D2:], ALU.add))
            dve.wait_ge(s_trans, 7)
            step(cast(rowz[:, 0:4, :].rearrange("h k p -> h (k p)"), PS[0:HEADS, 2, 0:4 * P]))
            step(dve.memset(prod, 1.0))
            step(dve.tensor_tensor_scan(out=inv_in[:], data0=same[:], data1=prod, initial=0.0, op0=ALU.mult, op1=ALU.add))
            dve.nop().then_inc(s_keys, 1)
            dve.wait_ge(s_trans, 8)
            step(cast(col(CNT_C), PS[:, 3, 0:1]))
            step(dve.scalar_tensor_tensor(out=inv_in[:], in0=first_seg[:], scalar=col(CNT_C), in1=inv_in[:], op0=ALU.mult, op1=ALU.add))
            dve.nop().then_inc(s_keys, 1)
            dve.wait_ge(s_trans, 9)
            step(dve.reciprocal(rs_in[:], rs_in[:]))
            step(dve.reciprocal(inv_in[:], inv_in[:]))
            at_first_tail(col(INV_FT), inv_in[:])
            at_first_tail(col(RSIN_FT), rs_in[:])
            barrier()

            Rh = R[:, :, :].bitcast(F16)

            def hot(b):
                return Rh[:, b, 0:HCOLS * HSLOT].rearrange("p (k s) -> p k s", k=HCOLS)

            with dve.Fori(0, HTURNS) as it:
                for b in range(2):
                    step.reset()
                    dve.wait_ge(s_binned, 2 * it + b + 1)
                    step(cast(fw[:, b, :, :], EE[:, 3:9, bass.ds((2 * it + b) * HCOLS, HCOLS)]))
                    h1 = HI + 1
                    for k in range(HCOLS):
                        sc = [fw[:, b, f, k:k + 1] for f in range(6)]
                        o = hot(b)[:, k, :]
                        ts(o[:, 0:h1], iota_h[:], sc[0], None, ALU.is_equal)
                        ts(o[:, h1:2 * h1], iota_h[:], sc[2], sc[4], ALU.is_equal, ALU.mult)
                        ts(o[:, 2 * h1:3 * h1], iota_h[:], sc[2], sc[5], ALU.is_equal, ALU.mult)
                        ts(o[:, 3 * h1:3 * h1 + 256], iota_h[:, 0:256], sc[1], None, ALU.is_equal)
                        last = ts(o[:, 3 * h1 + 256:], iota_h[:, 0:256], sc[3], None, ALU.is_equal)
                    last.then_inc(s_hot, 1)
            dve.wait_ge(s_binned, 2 * HTURNS + 3)
            step.reset()
            for l in range(LOB):
                step(cast(info[:, l, :, 1], PS[:, l, 0:HI]))
                step(cast(info[:, l, :, 0], PS[:, LOB + l, 0:HI]))
                step(dve.scalar_tensor_tensor(out=info[:, l, :, 0], in0=info[:, l, :, 0], scalar=256.0,
                                              in1=PS[:, 2 * LOB + l, 0:HI], op0=ALU.mult, op1=ALU.add))
            dve.nop().then_inc(s_bins, 1)
            barrier()

            def norm(x_in, h_out, n, ln, parts=P):
                xc, sq = cut(XC[0:parts, 0:n * D]), cut(SQ[0:parts, 0:n * D])
                mean, var, dev, inv = (st[0:parts, k, 0:n] for k in range(4))
                step(dve.tensor_reduce(mean, cut(x_in), AX_X, ALU.add))
                step(ts(mean, mean, 1.0 / D, None, ALU.mult))
                tt(xc, cut(x_in), over(mean, D), ALU.subtract).then_inc(s_xc, 1)
                dve.wait_ge(s_sq, ln)
                dve.tensor_reduce(var, sq, AX_X, ALU.add).then_inc(s_var, 1)
                dve.wait_ge(s_std, ln)
                step(dve.reciprocal(inv, dev))
                return dve.scalar_tensor_tensor(out=cut(h_out), in0=xc, scalar=0.0, in1=over(inv, D), op0=ALU.max, op1=ALU.mult)

            def scans(out_, in_, flags, initial, width, n=C, backward=False):
                order = slice(None, None, -1) if backward else slice(None)
                for f in range(width):
                    last = dve.tensor_tensor_scan(out=out_[:, order, f], data0=flags[:, order], data1=in_[:, order, f],
                                                  initial=initial[:, f:f + 1], op0=ALU.mult, op1=ALU.add)
                return last

            CD = C * D

            def wait_done(phase, i):
                dve.wait_ge(s_done, before[phase, "done"] + 1 + i)
                step(dve.memset(cols[:, SCR:SCR + 1], 0.0))

            def source(i, it, b):
                step.reset()
                dve.wait_ge(s_ld[b], before["source", "ld"] + 16 * (it + 1))
                ln = before["source", "ln"] + 1 + 2 * i
                norm(XB[:, b, :], G[:, b, :], C, ln).then_inc(s_ready, 1)
                dve.wait_ge(s_ready, before["source", "ready"] + 1 + i)
                which = cut(SQ[:, 0:C * RELS], RELS)
                step(tt(which, over(etf[:, bass.ds(i * C, C)], RELS), iota_r[:].unsqueeze(1).broadcast_to([P, C, RELS]), ALU.is_equal))
                for j in range(C):
                    dve.wait_ge(s_mturned, 2 * (i * C + j) + 2)
                    tt(cut(O[:, j % 2, CD:CD + RELS * D]), G[:, b, j * D:(j + 1) * D].unsqueeze(1).broadcast_to([P, RELS, D]),
                       over(which[:, j, :], D), ALU.mult).then_inc(s_mask, 1)
                dve.wait_ge(s_out, before["source", "group"] + AHEAD + 3 * GROUPS * (i + 1))
                step(tt(XB[:, b, :], XB[:, b, :], O[:, b, 0:CD], ALU.add))
                step(norm(XB[:, b, :], O[:, b, 0:CD], C, ln + 1))
                dve.wait_ge(s_mout, AHEAD + GROUPS * (i + 1))
                scans(cut(R[:, b, CD:]), cut(R[:, b, 0:CD]), same[:, bass.ds(i * C, C)], R[:, 1 - b, 2 * CD - D:2 * CD], D).then_inc(s_done, 1)
                wait_done("source", i)

            paired(dve, TURNS, source)
            step.reset()
            dve.wait_ge(s_carry, 1)
            step(cast(VB[:], PS[:, 5, 0:D]))
            barrier()

            def dest(i, it, b):
                step.reset()
                dve.wait_ge(s_ld[b], before["dest", "ld"] + 32 * (it + 1))
                step(tt(cut(SQ[:]), VB[:].unsqueeze(1).broadcast_to([P, C, D]), over(first_tail[:, bass.ds(i * C, C)], D), ALU.mult))
                step(tt(XB[:, b, :], XB[:, b, :], R[:, b, 0:CD], ALU.add))
                step(tt(XB[:, b, :], XB[:, b, :], SQ[:], ALU.add))
                norm(XB[:, b, :], G[:, b, :], C, before["dest", "ln"] + 1 + i).then_inc(s_done, 1)
                wait_done("dest", i)

            paired(dve, TURNS, dest)
            barrier()

            def nodes(i, it, b):
                step.reset()
                dve.wait_ge(s_ld[b], before["nodes", "ld"] + 16 * (it + 1))
                xb = XB[0:NP_, b, 0:NC * D]
                norm(xb, G[0:NP_, b, 0:NC * D], NC, before["nodes", "ln"] + 1 + i, NP_).then_inc(s_ready, 1)
                step(tt(cut(xb), cut(xb), bias2b[0:NP_].unsqueeze(1).broadcast_to([NP_, NC, D]), ALU.add))
                dve.wait_ge(s_out, before["nodes", "group"] + AHEAD + 3 * NGROUPS * (i + 1))
                tt(xb, xb, O[0:NP_, b, 0:NC * D], ALU.add).then_inc(s_done, 1)

            paired(dve, NCHUNKS // 2, nodes)
            step.reset()
            barrier()
            dve.wait_ge(s_infoc, 1)
            step(ts(tmp[:], EE[:, 0, :], 0.0, FAR, ALU.is_equal, ALU.mult))
            step(ts(EE[:, 0, :], EE[:, 0, :], 1.0, None, ALU.subtract))
            step(tt(tmp[:], tmp[:], EE[:, 0, :], ALU.add))
            step(cast(srcq[:], tmp[:]))
            step(cast(EE[:, 2, :], dsti[:]))
            step(tt(EE[:, 2, :], EE[:, 2, :], tail[:], ALU.mult))
            step(dve.scalar_tensor_tensor(out=EE[:, 2, :], in0=rest[:], scalar=FAR, in1=EE[:, 2, :], op0=ALU.mult, op1=ALU.add))
            step(cast(dstq[:], EE[:, 2, :]))
            step(ts(EE[:, 1, :], EE[:, 1, :], 1.0, None, ALU.max))
            ts(EE[:, 5, :], EE[:, 5, :], 1.0, None, ALU.max).then_inc(s_prep, 1)
            dve.wait_ge(s_patch, 16)
            step(ts(cols[:, SCR:SCR + 1], PG[:, 0, 0:1], 1.0, 0.0, ALU.subtract, ALU.max))
            cast(coli(IX_LAST), cols[:, SCR:SCR + 1]).then_inc(s_last, 1)
            dve.wait_ge(s_prep, 2)
            step(dve.reciprocal(rs_src[:], rs_src[:]))
            step(dve.reciprocal(rs_dst[:], rs_dst[:]))
            for values, k in ((rs_dst, RSDST_FT),):
                step(tt(tmp[:], values[:], first_tail[:], ALU.mult))
                step(dve.tensor_reduce(col(k), tmp[:], AX_X, ALU.add))
            step(ts(col(SCR), col(SCR), 1.0, -1.0, ALU.min, ALU.add))
            tt(col(SCR), col(SCR), bias1c[:], ALU.max).then_inc(s_prep, 1)
            dve.wait_ge(s_carry, before["prep", "carry"] + 1)
            step(cast(cut(XC[:]), PS[:, 3, 0:D].unsqueeze(1).broadcast_to([P, C, D])))
            dve.nop().then_inc(s_prep, 1)
            barrier()

            def halves(b, n):
                both = cut(HH[:, b, 0:n * D2], D2)
                return both[:, :, 0:D], both[:, :, D:]

            def per_row(array, i, first, n):
                return over(array[:, bass.ds(i * C, C)] if n == C else col(first), D)

            def operands(k, i, b, n):
                r, (left, right) = cut(R[:, b, 0:n * D]), halves(b, n)
                if k < 3:
                    return tt(left, r, per_row(inv_in, i, INV_FT, n), ALU.mult)
                step(tt(right, right, per_row(rs_dst, i, RSDST_FT, n), ALU.mult))
                step(tt(right, right, r, ALU.mult))
                return cast(left, r)

            def new_state(k, layer, i, b, n):
                o, xb = O[:, b, 0:n * D], XB[:, b, 0:n * D]
                if k == 3:
                    step(tt(cut(o), cut(o), per_row(rs_in, i, RSIN_FT, n), ALU.mult))
                step(tt(xb, xb, o, ALU.add))
                norm(xb, o, n, before[layer, "ln"] + 1 + i).then_inc(s_done, 1)

            for k, layer in enumerate(LAYERS):
                normed = k >= 2

                def gathered(i, it, b):
                    step.reset()
                    dve.wait_ge(s_ld[b], before[layer, "ld"] + (1 + normed) * 16 * (it + 1))
                    step(dve.memset(col(SCR), 0.0))
                    dve.wait_ge(s_g[b], before[layer, "gath"] + 16 * C * (it + 1))
                    if k == 3:
                        step(tt(cut(G[:, b, :]), cut(G[:, b, :]), over(rs_src[:, bass.ds(i * C, C)], D), ALU.mult))
                    scans(cut(R[:, b, 0:CD]), cut(G[:, b, :]), same[:, bass.ds(i * C, C)], R[:, 1 - b, CD - D:CD], D).then_inc(s_scan, 1)
                    dve.wait_ge(s_scan, before[layer, "scan"] + 1 + i)
                    operands(k, i, b, C).then_inc(s_ready, 1)

                def finish(i, it, b):
                    dve.wait_ge(s_out, before[layer, "group"] + AHEAD + GROUPS * (i + 1))
                    new_state(k, layer, i, b, C)

                if normed:
                    gathered(0, 0, 0)

                    def turn(it):
                        gathered(2 * it + 1, it, 1)
                        finish(2 * it, it, 0)
                        gathered(2 * it + 2, it + 1, 0)
                        finish(2 * it + 1, it, 1)

                    with dve.Fori(0, TURNS - 1) as it:
                        turn(it)
                    gathered(CHUNKS - 1, TURNS - 1, 1)
                    finish(CHUNKS - 2, TURNS - 1, 0)
                    finish(CHUNKS - 1, TURNS - 1, 1)
                else:
                    paired(dve, TURNS, gathered)
                step.reset()
                barrier()
                dve.wait_ge(s_patch, before[layer, "patch"] + 16 * (2 + normed))
                dve.wait_ge(s_carry, before[layer, "carry"] + 1)
                step(tt(R[:, 0, 0:D], R[:, 0, 0:D], PS[:, 3, 0:D], ALU.add))
                operands(k, CHUNKS, 0, 1).then_inc(s_ready, 1)
                if normed:
                    dve.wait_ge(s_out, before[layer, "group"] + AHEAD + GROUPS * CHUNKS + 1)
                    new_state(k, layer, CHUNKS, 0, 1)
                barrier()

            def softmax(heads, X, Y, Z, at):
                pen_f, pen_b, pen = O[:, 0, 0:TILES], O[:, 0, TILES:2 * TILES], O[:, 0, 2 * TILES:3 * TILES]
                step(ts(pen_f, same[:], BIG, -BIG, ALU.mult, ALU.add))
                step(ts(pen_b, rest[:], BIG, -BIG, ALU.mult, ALU.add))
                for h in range(heads):
                    step(dve.tensor_tensor_scan(out=Y[:, h, :], data0=pen_f, data1=X[:, h, :], initial=-BIG, op0=ALU.add, op1=ALU.max))
                    step(dve.tensor_tensor_scan(out=Z[:, h, ::-1], data0=pen_b[:, ::-1], data1=X[:, h, ::-1], initial=-BIG, op0=ALU.add, op1=ALU.max))
                step(cast(tz[:, 0, 0:heads], Y[:, 0:heads, TILES - 1]))
                cast(tz[:, 1, 0:heads], Z[:, 0:heads, 0]).then_inc(s_sm, 1)
                dve.wait_ge(s_sm, at + 2)
                row = lambda k: rowz[0:heads, k, :]
                step(cast(rowz[0:heads, 4:6, :].rearrange("h k p -> h (k p)"), PS[0:heads, 0, 0:2 * P]))
                step(dve.tensor_tensor_scan(out=row(6), data0=row(0), data1=row(4), initial=-BIG, op0=ALU.add, op1=ALU.max))
                step(dve.tensor_tensor_scan(out=row(7)[:, ::-1], data0=row(1)[:, ::-1], data1=row(5)[:, ::-1], initial=-BIG, op0=ALU.add, op1=ALU.max))
                step(dve.memset(rowz[0:heads, 4:6, :], -BIG))
                step(tt(row(4)[:, 1:], row(6)[:, 0:P - 1], row(2)[:, 1:], ALU.add))
                tt(row(5)[:, 0:P - 1], row(7)[:, 1:], row(3)[:, 0:P - 1], ALU.add).then_inc(s_sm, 1)
                dve.wait_ge(s_sm, at + 4)
                step(cast(tz[:, 2:4, 0:heads], PS[:, 1, 0:2 * HEADS].rearrange("p (k h) -> p k h", k=2)[:, :, 0:heads]))
                step(tt(Y[:, 0:heads, :], Y[:, 0:heads, :], Z[:, 0:heads, :], ALU.max))
                for seg, k in ((first_seg, 2), (last_seg, 3)):
                    step(ts(pen, seg[:], BIG, -BIG, ALU.mult, ALU.add))
                    for h in range(heads):
                        step(dve.scalar_tensor_tensor(out=Y[:, h, :], in0=pen, scalar=tz[:, k, h:h + 1], in1=Y[:, h, :], op0=ALU.add, op1=ALU.max))
                tt(X[:, 0:heads, :], X[:, 0:heads, :], Y[:, 0:heads, :], ALU.subtract).then_inc(s_sm, 1)
                dve.wait_ge(s_sm, at + 6)
                for h in range(heads):
                    step(dve.tensor_tensor_scan(out=Z[:, h, :], data0=same[:], data1=X[:, h, :], initial=0.0, op0=ALU.mult, op1=ALU.add))
                cast(tz[:, 4, 0:heads], Z[:, 0:heads, TILES - 1]).then_inc(s_sm, 1)
                dve.wait_ge(s_sm, at + 8)
                step(cast(tz[:, 6, 0:heads], PS[:, 2, 0:heads]))
                for h in range(heads):
                    step(dve.scalar_tensor_tensor(out=Z[:, h, :], in0=first_seg[:], scalar=tz[:, 6, h:h + 1], in1=Z[:, h, :], op0=ALU.mult, op1=ALU.add))
                step(ts(Z[:, 0:heads, :], Z[:, 0:heads, :], 1e-16, None, ALU.add))
                step(dve.reciprocal(Z[:, 0:heads, :], Z[:, 0:heads, :]))
                step(tt(Y[:, 0:heads, :], Z[:, 0:heads, :], first_tail[:].unsqueeze(1).broadcast_to([P, heads, TILES]), ALU.mult))
                step(dve.tensor_reduce(tz[:, 5, 0:heads], Y[:, 0:heads, :], AX_X, ALU.add))

            def back(i):
                return i * (-1) + (CHUNKS - 1)

            dve.wait_ge(s_patch, before["att1", "patch"] + 16)
            dve.sem_inc(s_scored, AHEAD)
            step(cast(HH[:, 1, D:D2], VB[:]))

            def spread(phase, i, it, b, to, initial):
                dve.wait_ge(s_g[b], before[phase, "gath"] + 16 * C * (it + 1))
                step(dve.memset(col(SCR), 0.0))
                dve.wait_ge(s_ld[b], before[phase, "ld"] + 16 * (it + 1))
                at = bass.ds(back(i) * C, C)
                step(tt(cut(XB[:, b, :]), cut(XB[:, b, :]), over(tail[:, at], D), ALU.mult))
                step(cast(st[:, 0, :], rest[:, at]))
                return scans(to, cut(XB[:, b, :]), st[:, 0, :], initial, D, backward=True)

            def operands1(i, it, b):
                step.reset()
                spread("att1", i, it, b, halves(b, C)[1], HH[:, 1 - b, D:D2]).then_inc(s_ready, 1)
                dve.wait_ge(s_ready, before["att1", "ready"] + 1 + i)
                step(dve.memset(col(SCR), 0.0))

            def scores1(i, it, b):
                for g in range(GROUPS):
                    k = (g + b * GROUPS) % 2
                    s, l = SX[:, k, 0:512], SX[:, k, 512:1024]
                    dve.wait_ge(s_out, before["att1", "group"] + AHEAD + GROUPS * i + g + 1)
                    step(dve.scalar_tensor_tensor(out=l, in0=s, scalar=0.2, in1=s, op0=ALU.mult, op1=ALU.max))
                    step(tt(cut(l, D2), cut(l, D2), attb1[:].unsqueeze(1).broadcast_to([P, G4, D2]), ALU.mult))
                    dve.tensor_reduce(Ea[:, :, bass.ds(back(i) * C + g * G4, G4)].rearrange("p h j -> p j h"),
                                      l.rearrange("p (j h c) -> p j h c", j=G4, h=HEADS), AX_X, ALU.add).then_inc(s_scored, 1)
                dve.wait_ge(s_scored, AHEAD + GROUPS * i + GROUPS)
                step(dve.memset(col(SCR), 0.0))

            operands1(0, 0, 0)
            with dve.Fori(0, TURNS - 1) as it:
                operands1(2 * it + 1, it, 1)
                scores1(2 * it, it, 0)
                operands1(2 * it + 2, it + 1, 0)
                scores1(2 * it + 1, it, 1)
            operands1(CHUNKS - 1, TURNS - 1, 1)
            scores1(CHUNKS - 2, TURNS - 1, 0)
            scores1(CHUNKS - 1, TURNS - 1, 1)
            step.reset()
            barrier()
            softmax(HEADS, Ea, Eb, Ec, 0)
            barrier()

            def weighted(i, it, b):
                step.reset()
                dve.wait_ge(s_ld[b], before["sum1", "ld"] + 16 * (it + 1))
                at = bass.ds(i * C, C)
                rows4 = lambda t: t.rearrange("p (j h c) -> p j h c", h=HEADS, c=D2 // HEADS)
                per_head = lambda e: e[:, :, at].rearrange("p h j -> p j h").unsqueeze(3).broadcast_to([P, C, HEADS, D2 // HEADS])
                step(tt(rows4(HH[:, b, :]), rows4(HH[:, b, :]), per_head(Ea), ALU.mult))
                scans(cut(R[:, b, :], D2), cut(HH[:, b, :], D2), same[:, at], R[:, 1 - b, 2 * CD - D2:], D2).then_inc(s_scan, 1)
                dve.wait_ge(s_scan, before["sum1", "scan"] + 1 + i)
                tt(rows4(HH[:, b, :]), rows4(R[:, b, :]), per_head(Ec), ALU.mult).then_inc(s_ready, 1)

            def elu(i, b, g, n=G4):
                k = (g + b * GROUPS) % 2
                at = GROUPS * i + g
                dve.wait_ge(s_exp, at + 1)
                step(ts(SX[:, k, 0:n * P], SX[:, k, 0:n * P], 1.0, -1.0, ALU.min, ALU.add))
                dve.wait_ge(s_mult, before["sum1", "group"] + GROUPS * i + g + 1)
                dve.scalar_tensor_tensor(out=AT[:, k, 0:n * P], in0=PS[:, 4 + k, 0:n * P], scalar=bias1c[:], in1=SX[:, k, 0:n * P],
                                         op0=ALU.add, op1=ALU.max).then_inc(s_elu, 1)

            def elus(i, it, b):
                for g in range(GROUPS):
                    elu(i, b, g)

            dve.sem_inc(s_elu, AHEAD)
            weighted(0, 0, 0)
            with dve.Fori(0, TURNS - 1) as it:
                weighted(2 * it + 1, it, 1)
                elus(2 * it, it, 0)
                weighted(2 * it + 2, it + 1, 0)
                elus(2 * it + 1, it, 1)
            weighted(CHUNKS - 1, TURNS - 1, 1)
            elus(CHUNKS - 2, TURNS - 1, 0)
            elus(CHUNKS - 1, TURNS - 1, 1)
            step.reset()
            barrier()
            dve.wait_ge(s_patch, before["sum1", "patch"] + 16)
            dve.wait_ge(s_carry, before["sum1", "carry"] + 1)
            step(tt(R[:, 0, 0:D2], R[:, 0, 0:D2], PS[:, 3, 0:D2], ALU.add))
            tt(cut(HH[:, 0, 0:D2], D2 // HEADS), cut(R[:, 0, 0:D2], D2 // HEADS), over(tz[:, 5, :], D2 // HEADS), ALU.mult).then_inc(s_ready, 1)
            elu(CHUNKS, 0, 0, 1)
            barrier()

            dve.wait_ge(s_patch, before["att2", "patch"] + 16)
            step(cast(HH[:, 1, 0:D], VB[:]))

            def scores2(i, it, b):
                step.reset()
                one, two = HH[:, b, 0:CD], HH[:, b, CD:]
                spread("att2", i, it, b, cut(one), HH[:, 1 - b, 0:D]).then_inc(s_scan2, 1)
                dve.wait_ge(s_scan2, i + 1)
                step(tt(two, G[:, b, :], one, ALU.add))
                step(dve.scalar_tensor_tensor(out=two, in0=two, scalar=0.2, in1=two, op0=ALU.mult, op1=ALU.max))
                step(tt(cut(two), cut(two), attb2[:].unsqueeze(1).broadcast_to([P, C, D]), ALU.mult))
                dve.tensor_reduce(Eb[:, 0, bass.ds(back(i) * C, C)], cut(two), AX_X, ALU.add).then_inc(s_done, 1)

            paired(dve, TURNS, scores2)
            step.reset()
            barrier()
            softmax(1, Eb, Ea, Ec, 8)
            barrier()

            def result(r, o, xb, n, inverse):
                step(tt(cut(o), cut(r), inverse, ALU.mult))
                step(tt(cut(o), cut(o), bias2b[:].unsqueeze(1).broadcast_to([P, n, D]), ALU.add))
                return tt(o, o, xb, ALU.add)

            def weighted2(i, it, b):
                step.reset()
                dve.wait_ge(s_ld[b], before["sum2", "ld"] + 32 * (it + 1))
                at = bass.ds(i * C, C)
                step(tt(cut(G[:, b, :]), cut(G[:, b, :]), over(Eb[:, 0, at], D), ALU.mult))
                scans(cut(R[:, b, 0:CD]), cut(G[:, b, :]), same[:, at], R[:, 1 - b, CD - D:CD], D).then_inc(s_scan, 1)
                dve.wait_ge(s_scan, before["sum2", "scan"] + 1 + i)
                result(R[:, b, 0:CD], O[:, b, 0:CD], XB[:, b, :], C, over(Ec[:, 0, at], D)).then_inc(s_ready, 1)

            paired(dve, TURNS, weighted2)
            step.reset()
            barrier()
            dve.wait_ge(s_patch, before["sum2", "patch"] + 32)
            dve.wait_ge(s_carry, before["sum2", "carry"] + 1)
            step(tt(R[:, 0, 0:D], R[:, 0, 0:D], PS[:, 3, 0:D], ALU.add))
            result(R[:, 0, 0:D], O[:, 0, 0:D], XB[:, 0, 0:D], 1, over(tz[:, 5, 0:1], D)).then_inc(s_sm, 1)
            barrier()

        @block.tensor
        def _(pe):
            barrier = Barrier(pe)
            pe.wait_ge(s_const, 2)
            pe.wait_ge(s_keys, 1)
            pe.wait_ge(s_cols, 1)
            pe.matmul(PS[:, 0, 0:P], cols[:, DF:DF + 1].broadcast_to([P, P]), ident[:], start=True, stop=True).then_inc(s_trans, 1)
            pe.wait_ge(s_w, 16 * WEIGHT_LOADS)
            pe.transpose(PS[:, 1, 0:P], SQ[:, 0:D2], ident[:]).then_inc(s_trans, 1)
            pe.transpose(PS[:, 1, P:2 * P], SQ[:, D2:2 * D2], ident[:]).then_inc(s_trans, 1)
            for k, c in enumerate((PEN_P, PEN_N, CAP_P, CAP_N)):
                pe.matmul(PS[0:HEADS, 2, k * P:(k + 1) * P], cols[:, c:c + 1].broadcast_to([P, HEADS]), ident[:],
                          start=True, stop=True).then_inc(s_trans, 1)
            pe.wait_ge(s_keys, 2)
            pe.matmul(PS[:, 3, 0:1], CARRY[:], inv_in[:, TILES - 1:TILES], start=True, stop=True).then_inc(s_trans, 1)
            barrier()
            for k in range(3 * LOB):
                pe.matmul(PS[:, k, 0:HI + 1], zeroh[:, 0:P], zeroh[:, 0:HI + 1], start=True, stop=False, skip_group_check=True)
            pe.matmul(PS[:, 6, 0:1], zeroh[:, 0:P], zeroh[:, 0:1], start=True, stop=True).then_inc(s_binned, 2)
            Rh = R[:, :, :].bitcast(F16)
            h1 = HI + 1
            with pe.Fori(0, HTURNS) as it:
                for b in range(2):
                    hot = Rh[:, b, 0:HCOLS * HSLOT].rearrange("p (k s) -> p k s", k=HCOLS)
                    pe.wait_ge(s_hot, 2 * it + b + 1)
                    for k in range(HCOLS):
                        o = hot[:, k, :]
                        for l in range(LOB):
                            lo_src = o[:, 3 * h1 + l * P:3 * h1 + (l + 1) * P]
                            lo_dst = o[:, 3 * h1 + 256 + l * P:3 * h1 + 256 + (l + 1) * P]
                            pe.matmul(PS[:, l, 0:h1], lo_src, o[:, 0:h1], start=False, stop=False, skip_group_check=True)
                            pe.matmul(PS[:, LOB + l, 0:h1], lo_dst, o[:, h1:2 * h1], start=False, stop=False, skip_group_check=True)
                            last = pe.matmul(PS[:, 2 * LOB + l, 0:h1], lo_dst, o[:, 2 * h1:3 * h1], start=False, stop=False, skip_group_check=True)
                    last.then_inc(s_binned, 1)
            for k in range(3 * LOB):
                last = pe.matmul(PS[:, k, 0:HI + 1], zeroh[:, 0:P], zeroh[:, 0:HI + 1], start=False, stop=True, skip_group_check=True)
            last.then_inc(s_binned, 1)
            barrier()

            class Lone:

                def __init__(self, phase, groups, parts):
                    self.phase, self.groups, self.parts = phase, groups, parts

                def turn(self, i, b, u):
                    s, g = divmod(u, self.groups)
                    if s == 0:
                        pe.wait_ge(s_ready, before[self.phase, "ready"] + 1 + i)
                    else:
                        pe.wait_ge(s_out, before[self.phase, "group"] + AHEAD + 1 + 3 * self.groups * i + u - self.groups)
                    of = (G[:, b, :], HH[:, b, 0:C * D], HH[:, b, C * D:])[s]
                    k = (u + b * 3 * self.groups) % 2
                    for q in range(2):
                        last = pe.transpose(PS[:, 4 + k, q * P:q * P + self.parts],
                                            of[0:self.parts, (2 * g + q) * D2:(2 * g + q + 1) * D2], ident[0:self.parts, 0:self.parts])
                    last.then_inc(s_turned, 1)

                def multiply(self, i, b, u):
                    s = u // self.groups
                    k = (u + b * 3 * self.groups) % 2
                    n = before[self.phase, "group"] + 3 * self.groups * i + u
                    pe.wait_ge(s_copied, n + 1)
                    pe.wait_ge(s_out, n + 1)
                    for q in range(2):
                        to = PS[0:self.parts, 6 + k, q * P:(q + 1) * P]
                        pe.matmul(to, AT[:, k, q * P:q * P + self.parts], WS[:, s, :], start=True, stop=False, skip_group_check=True)
                        last = pe.matmul(to, ones[:, 0:self.parts], BS[:, s, :], start=False, stop=True, skip_group_check=True)
                    last.then_inc(s_mult, 1)

            pe.sem_inc(s_mult, AHEAD)
            pe.sem_inc(s_mturned, 2 * AHEAD)
            pe.sem_inc(s_mmult, AHEAD)
            lone_steps = Lone("source", GROUPS, P)

            def mask_turn(i, j):
                pe.wait_ge(s_mask, i * C + j + 1)
                for h in range(2):
                    pe.wait_ge(s_mcopied, 2 * (i * C + j) + h + 1)
                    for r in range(RELS // 4):
                        at = C * D + (h * RELS // 4 + r) * D2
                        last = pe.transpose(PS[:, h, r * P:(r + 1) * P], O[:, j % 2, at:at + D2], ident[:])
                    last.then_inc(s_mturned, 1)

            def mask_multiply(i, b, j):
                pe.wait_ge(s_mcopied, 2 * (i * C + j) + 2 + AHEAD)
                if j % G4 == 0:
                    pe.wait_ge(s_mout, i * GROUPS + j // G4 + 1)
                to = PS[:, 2 + (j // G4 + b) % 2, (j % G4) * D:(j % G4 + 1) * D]
                for r in range(RELS // 2):
                    last = pe.matmul(to, SX[:, j % 2, r * P:(r + 1) * P], W0[:, r, :], start=(r == 0), stop=(r == RELS // 2 - 1),
                                     skip_group_check=True)
                last.then_inc(s_mmult, 1)

            def source(i, it, b):
                for u in range(C + 1):
                    if u < 3 * GROUPS:
                        lone_steps.turn(i, b, u)
                    if u < C:
                        mask_turn(i, u)
                    if 1 <= u <= 3 * GROUPS:
                        lone_steps.multiply(i, b, u - 1)
                    if u >= 1:
                        mask_multiply(i, b, u - 1)

            paired(pe, TURNS, source)
            pe.wait_ge(s_done, before["source", "done"] + CHUNKS)
            pe.matmul(PS[:, 5, 0:D], CARRY[:], R[:, 1, 2 * C * D - D:2 * C * D], start=True, stop=True).then_inc(s_carry, 1)
            barrier()
            barrier()
            node_steps = Lone("nodes", NGROUPS, NP_)

            def nodes(i, it, b):
                for u in range(3 * NGROUPS + 1):
                    if u < 3 * NGROUPS:
                        node_steps.turn(i, b, u)
                    if u >= 1:
                        node_steps.multiply(i, b, u - 1)

            paired(pe, NCHUNKS // 2, nodes)
            barrier()
            pe.wait_ge(s_prep, 3)
            pe.matmul(PS[:, 3, 0:D], cols[:, SCR:SCR + 1].broadcast_to([P, P]), WG2[:, 0:D], start=True, stop=False)
            pe.matmul(PS[:, 3, 0:D], ones[:], BG2[:, 0:D], start=False, stop=True).then_inc(s_carry, 1)
            barrier()

            def turn(phase, i, b, g, n=G4):
                pe.wait_ge(s_ready, before[phase, "ready"] + 1 + i)
                k = (g + b * GROUPS) % 2
                for q in range(n):
                    last = pe.transpose(PS[:, 4 + k, q * P:(q + 1) * P], HH[:, b, (g * G4 + q) * D2:(g * G4 + q + 1) * D2], ident[:])
                last.then_inc(s_turned, 1)

            def multiply(phase, i, b, g, weights, bias, width, n=G4, to_bank=None, ready=None):
                k = (g + b * GROUPS) % 2
                at = before[phase, "group"] + GROUPS * i + g
                if ready is None:
                    pe.wait_ge(s_copied, before[phase, "group"] + GROUPS * i + g + 1)
                else:
                    pe.wait_ge(*ready(i, g))
                pe.wait_ge(s_out, at + 1)
                for q in range(n):
                    if width == 2 * D2:
                        to = PS[:, 2 * k + q // 2, (q % 2) * width:(q % 2 + 1) * width]
                    else:
                        to = PS[:, 6 + k, q * width:(q + 1) * width]
                    last = pe.matmul(to, AT[:, k, q * P:(q + 1) * P], weights, start=True, stop=bias is None, skip_group_check=True)
                    if bias is not None:
                        last = pe.matmul(to, ones[:], bias, start=False, stop=True, skip_group_check=True)
                last.then_inc(s_mult, 1)

            def products(phase, *how, **more):
                def body(i, it, b):
                    for g in range(GROUPS + 1):
                        if g < GROUPS:
                            turn(phase, i, b, g)
                        if g >= 1:
                            multiply(phase, i, b, g - 1, *how, **more)
                return body

            def carry(phase, width, at):
                pe.matmul(PS[:, 3, 0:width], CARRY[:], R[:, 1, at - width:at], start=True, stop=True).then_inc(s_carry, 1)

            for k, layer in enumerate(LAYERS):
                how = (WD[:, k, :], BS[:, k, 0:D], D) if k < 3 else (W12[:], None, D)
                paired(pe, TURNS, products(layer, *how))
                barrier()
                carry(layer, D, C * D)
                turn(layer, CHUNKS, 0, 0, 1)
                multiply(layer, CHUNKS, 0, 0, *how, n=1)
                barrier()
            paired(pe, TURNS, products("att1", WG1[:], BG1[:], 2 * D2))
            barrier()

            def softmax(heads, at):
                pe.wait_ge(s_sm, at + 1)
                for k in range(2):
                    last = pe.transpose(PS[0:heads, 0, k * P:(k + 1) * P], tz[:, k, 0:heads], ident[:])
                last.then_inc(s_sm, 1)
                pe.wait_ge(s_sm, at + 3)
                for k in range(2):
                    last = pe.transpose(PS[:, 1, k * HEADS:k * HEADS + heads], rowz[0:heads, 4 + k, :], ident[0:heads, 0:heads])
                last.then_inc(s_sm, 1)
                pe.wait_ge(s_sm, at + 7)
                pe.matmul(PS[:, 2, 0:heads], CARRY[:], tz[:, 4, 0:heads], start=True, stop=True).then_inc(s_sm, 1)

            softmax(HEADS, 0)
            barrier()
            how = (WG2[:], BG2[:], D2)
            ready = lambda i, g: (s_elu, GROUPS * i + g + 1 + AHEAD)
            paired(pe, TURNS, products("sum1", *how, ready=ready))
            barrier()
            carry("sum1", D2, 2 * C * D)
            turn("sum1", CHUNKS, 0, 0, 1)
            multiply("sum1", CHUNKS, 0, 0, *how, n=1, ready=ready)
            barrier()
            barrier()
            softmax(1, 8)
            barrier()
            barrier()
            carry("sum2", D, C * D)
            barrier()

        @block.scalar
        def _(act):
            barrier = Barrier(act)
            act.wait_ge(s_keys, 3)
            act.activation(rs_in[:], inv_in[:], ACT.Sqrt).then_inc(s_trans, 1)
            barrier()
            barrier()

            def norm(n, ln, parts=P):
                act.wait_ge(s_xc, ln)
                act.activation(SQ[0:parts, 0:n * D], XC[0:parts, 0:n * D], ACT.Square).then_inc(s_sq, 1)
                act.wait_ge(s_var, ln)
                act.activation(st[0:parts, 2, 0:n], st[0:parts, 1, 0:n], ACT.Sqrt, bias=epsc[0:parts, :], scale=1.0 / D).then_inc(s_std, 1)

            class Lone:

                def __init__(self, phase, groups, parts):
                    self.phase, self.groups, self.parts = phase, groups, parts

                def n(self, i, u):
                    return before[self.phase, "group"] + 3 * self.groups * i + u

                def turned(self, i, b, u):
                    k = (u + b * 3 * self.groups) % 2
                    act.wait_ge(s_turned, self.n(i, u) + 1)
                    act.wait_ge(s_mult, self.n(i, u) + 1)
                    if self.parts == P:
                        act.copy(AT[:, k, 0:2 * P], PS[:, 4 + k, 0:256]).then_inc(s_copied, 1)
                    else:
                        act.copy(cut(AT[:, k, 0:2 * P], P)[:, :, 0:self.parts], cut(PS[:, 4 + k, 0:256], P)[:, :, 0:self.parts]
                                 ).then_inc(s_copied, 1)

                def out(self, i, b, u):
                    s, g = divmod(u, self.groups)
                    k = (u + b * 3 * self.groups) % 2
                    act.wait_ge(s_mult, self.n(i, u) + 1 + AHEAD)
                    to = (HH[:, b, 0:C * D], HH[:, b, C * D:], O[:, b, 0:C * D])[s]
                    act.activation(to[0:self.parts, g * 256:(g + 1) * 256], PS[0:self.parts, 6 + k, 0:256],
                                   ACT.Relu if s < 2 else ACT.Identity).then_inc(s_out, 1)

            act.sem_inc(s_out, AHEAD)
            act.sem_inc(s_mout, AHEAD)
            act.sem_inc(s_mcopied, AHEAD)
            lone_steps = Lone("source", GROUPS, P)

            def mask_copy(i, j):
                act.wait_ge(s_mmult, i * C + j + 1)
                for h in range(2):
                    act.wait_ge(s_mturned, 2 * (i * C + j) + h + 1 + 2 * AHEAD)
                    act.copy(SX[:, j % 2, h * 512:(h + 1) * 512], PS[:, h, :]).then_inc(s_mcopied, 1)

            def messages(i, b, g):
                act.wait_ge(s_mmult, i * C + (g + 1) * G4 + AHEAD)
                act.copy(R[:, b, g * 256:(g + 1) * 256], PS[:, 2 + (g + b) % 2, 0:256]).then_inc(s_mout, 1)

            def source(i, it, b):
                ln = before["source", "ln"] + 1 + 2 * i
                norm(C, ln)
                for u in range(C + 1):
                    if u < 3 * GROUPS:
                        lone_steps.turned(i, b, u)
                    if u < C:
                        mask_copy(i, u)
                    if 1 <= u <= 3 * GROUPS:
                        lone_steps.out(i, b, u - 1)
                    if u >= G4 and u % G4 == 0:
                        messages(i, b, u // G4 - 1)
                norm(C, ln + 1)

            paired(act, TURNS, source)
            barrier()
            paired(act, TURNS, lambda i, it, b: norm(C, before["dest", "ln"] + 1 + i))
            barrier()
            node_steps = Lone("nodes", NGROUPS, NP_)

            def nodes(i, it, b):
                norm(NC, before["nodes", "ln"] + 1 + i, NP_)
                for u in range(3 * NGROUPS + 1):
                    if u < 3 * NGROUPS:
                        node_steps.turned(i, b, u)
                    if u >= 1:
                        node_steps.out(i, b, u - 1)

            paired(act, NCHUNKS // 2, nodes)
            barrier()
            act.wait_ge(s_prep, 1)
            act.activation(rs_src[:], EE[:, 1, :], ACT.Sqrt)
            act.activation(rs_dst[:], EE[:, 5, :], ACT.Sqrt)
            act.wait_ge(s_last, 1)
            act.activation(cols[:, SCR:SCR + 1], bias1c[:], ACT.Exp).then_inc(s_prep, 1)
            barrier()

            def copy(phase, i, b, g, n=G4):
                k = (g + b * GROUPS) % 2
                at = before[phase, "group"] + GROUPS * i + g
                act.wait_ge(s_turned, at + 1)
                act.wait_ge(s_mult, at + 1)
                act.copy(AT[:, k, 0:n * P], PS[:, 4 + k, 0:n * P]).then_inc(s_copied, 1)

            def multiplied(phase, i, g):
                act.wait_ge(s_mult, before[phase, "group"] + GROUPS * i + g + 1 + AHEAD)

            def out_rows(func):
                def put(phase, i, b, g, n=G4):
                    k = (g + b * GROUPS) % 2
                    multiplied(phase, i, g)
                    act.activation(O[:, b, g * 256:g * 256 + n * D], PS[:, 6 + k, 0:n * D], func).then_inc(s_out, 1)
                return put

            def products(phase, first, put, after=None):
                def body(i, it, b):
                    for g in range(GROUPS + 1):
                        if g < GROUPS:
                            first(phase, i, b, g)
                        if g >= 1:
                            put(phase, i, b, g - 1)
                    if after:
                        after(i)
                return body

            for k, layer in enumerate(LAYERS):
                put = out_rows(ACT.Relu if k < 2 else ACT.Identity)
                after = (lambda i, n=C: norm(n, before[layer, "ln"] + 1 + i)) if k >= 2 else None
                paired(act, TURNS, products(layer, copy, put, after))
                barrier()
                copy(layer, CHUNKS, 0, 0, 1)
                put(layer, CHUNKS, 0, 0, 1)
                if after:
                    after(CHUNKS, 1)
                barrier()

            def scores(phase, i, b, g):
                k = (g + b * GROUPS) % 2
                multiplied(phase, i, g)
                act.wait_ge(s_scored, GROUPS * i + g + 1)
                both = PS[:, 2 * k:2 * k + 2, :].rearrange("p k (j n) -> p (k j) n", n=2 * D2)
                act.copy(cut(SX[:, k, 0:512], D2), both[:, :, 0:D2])
                act.copy(cut(O[:, b, g * 512:(g + 1) * 512], D2), both[:, :, D2:]).then_inc(s_out, 1)

            paired(act, TURNS, products("att1", copy, scores))
            barrier()

            def softmax(X, heads, at):
                act.wait_ge(s_sm, at + 5)
                act.activation(X[:, 0:heads, :], X[:, 0:heads, :], ACT.Exp).then_inc(s_sm, 1)

            softmax(Ea, HEADS, 0)
            barrier()

            def exponential(phase, i, b, g, n=G4):
                k = (g + b * GROUPS) % 2
                act.wait_ge(s_turned, before[phase, "group"] + GROUPS * i + g + 1)
                act.wait_ge(s_elu, GROUPS * i + g + 1)
                act.activation(SX[:, k, 0:n * P], PS[:, 4 + k, 0:n * P], ACT.Exp, bias=bias1c[:]).then_inc(s_exp, 1)

            def second_operands(phase, i, b, g, n=G4):
                k = (g + b * GROUPS) % 2
                multiplied(phase, i, g)
                rows_ = cut(PS[:, 6 + k, 0:n * D2], D2)
                act.copy(cut(O[:, b, g * 256:g * 256 + n * D]), rows_[:, :, 0:D])
                act.copy(cut(O[:, b, C * D + g * 256:C * D + g * 256 + n * D]), rows_[:, :, D:]).then_inc(s_out, 1)

            paired(act, TURNS, products("sum1", exponential, second_operands))
            barrier()
            exponential("sum1", CHUNKS, 0, 0, 1)
            second_operands("sum1", CHUNKS, 0, 0, 1)
            barrier()
            barrier()
            softmax(Eb, 1, 8)
            barrier()
            barrier()
            barrier()


_INS = ['x', 'src', 'dst', 'edge_type_16', 'L0_gnn_weight', 'L1_gnn_Wl', 'L1_gnn_Wr', 'L1_gnn_b',
        'L2_gnn_weight1', 'L2_gnn_weight2', 'L3_gnn_Wl1', 'L3_gnn_bl1', 'L3_gnn_Wr1', 'L3_gnn_br1',
        'L3_gnn_att1', 'L3_gnn_bias1', 'L3_gnn_Wl2', 'L3_gnn_bl2', 'L3_gnn_Wr2', 'L3_gnn_br2',
        'L3_gnn_att2', 'L3_gnn_bias2']


def kernel(**inputs):
    import concourse.bacc as bacc
    from concourse.bass_utils import run_bass_kernel_spmd

    nc = bacc.Bacc("TRN2", target_bir_lowering=False, num_devices=1)
    arrays, args = {}, []
    for name in _INS:
        a = np.ascontiguousarray(inputs[name])
        arrays[f"in_{name}"] = a
        args.append(nc.dram_tensor(f"in_{name}", a.shape, mybir.dt.from_np(a.dtype), kind="ExternalInput").ap())
    out = nc.dram_tensor("out_nodes", (N, D), F32, kind="ExternalOutput").ap()
    build_program(nc, *args, out)
    return run_bass_kernel_spmd(nc, [arrays], core_ids=[0]).results[0]["out_nodes"]
```

```python
from contextlib import ExitStack

import numpy as np

import concourse.bass as bass
from concourse import mybir

ALU = mybir.AluOpType
ACT = mybir.ActivationFunctionType
F32 = mybir.dt.float32
F16 = mybir.dt.float16
I32 = mybir.dt.int32
AX_X = mybir.AxisListType.X

P = 128
N = 100000
E = 50000
D = 64
D2 = 2 * D
C = 28
CHUNKS = 14
TURNS = CHUNKS // 2
TILES = C * CHUNKS
ROWS = P * TILES
G4 = 4
GROUPS = C // G4
PC = 14
PCHUNKS = TILES // PC
NP_ = 125
NT = N // NP_
NC = 20
NCHUNKS = NT // NC
NGROUPS = NC // G4
RELS = 16
HEADS = 4
HI = (N >> 8) + 1
LOB = 2
PAD = 131071
FAR = 131072.0
BIG = 1.0e30
EPS = 1.0e-5
WEIGHT_LOADS = 35
HSLOT = 3 * (HI + 1) + 2 * 256
HCOLS = 4
HTURNS = TILES // (2 * HCOLS)
(DF, DL, JP, JN, WH, PEN_P, PEN_N, CAP_P, CAP_N, FT_ROW, FT_HAS, FT_OUT, INV_FT, RSIN_FT, RSDST_FT,
 MISS, SCR, CNT_C) = range(18)
IX_FT, IX_FTG, IX_LASTQ, IX_LAST, IX_OUT, SCR_I, SCR_J, NEG = range(8)


class Chain:

    def __init__(self, eng, sem):
        self.eng, self.sem, self.n = eng, sem, 0

    def reset(self):
        if self.n:
            self.eng.wait_ge(self.sem, 1)
        self.eng.sem_clear(self.sem)
        self.n = 0

    def __call__(self, ins):
        self.n += 1
        ins.then_inc(self.sem, 1)
        self.eng.wait_ge(self.sem, self.n)


def build_program(nc, x, src, dst, etype, w0, wl, wr, wb, w1, w2, gwl1, gbl1, gwr1, gbr1, gatt1, gbias1,
                  gwl2, gbl2, gwr2, gbr2, gatt2, gbias2, out):
    with ExitStack() as ctx:
        def sb(name, shape, dt=F32):
            return ctx.enter_context(nc.sbuf_tensor(name, shape, dt))

        def dram(name, shape, dt=F32):
            return nc.dram_tensor(name, shape, dt, kind="Internal").ap()

        def rows(name, width=D):
            return dram(name, [P, TILES * width])

        def by_row(t, width=D):
            return t.rearrange("p (t f) -> (p t) f", f=width)

        xsrc, xdst = rows("x_of_src"), rows("x_of_dst")
        lone = [rows(f"lone_state{k}") for k in range(4)]
        table = [rows(f"table{k}") for k in range(5)]
        total = [rows(f"total{k}") for k in range(5)]
        total_g1, total_g2 = rows("total_gat1", D2), rows("total_gat2")
        resid = [rows(f"resid{k}") for k in range(3)]
        xl1 = rows("xl1_of_src", D2)
        table_l2, table_r2 = rows("table_xl2"), rows("table_xr2")
        xl2 = rows("xl2_of_src")
        lone_xl2 = dram("lone_xl2", [P, C * D])
        dst_line = dram("dst_line", [ROWS + 2, 1], I32)
        node_info = dram("node_info", [P * LOB * HI, 2])

        sort_line, sort_rows = dram("sort_line", [P, 1]), dram("sort_rows", [ROWS, 4], I32)

        def edges(name, dt=F32):
            return sb(name, [P, TILES], dt)

        same, tail, rest = edges("same"), edges("tail"), edges("rest")
        first_seg, last_seg, first_tail = edges("first_seg"), edges("last_seg"), edges("first_tail")
        inv_in, rs_in, rs_src, rs_dst = edges("inv_in"), edges("rs_in"), edges("rs_src"), edges("rs_dst")
        etf = edges("etf")
        tmp = edges("tmp")
        srci, dsti = edges("srci", I32), edges("dsti", I32)
        srcq, dstq = edges("srcq", I32), edges("dstq", I32)
        EE = sb("EE", [P, 3 * HEADS, TILES])
        Ea, Eb, Ec = EE[:, 0:HEADS, :], EE[:, HEADS:2 * HEADS, :], EE[:, 2 * HEADS:, :]
        G = sb("G", [P, 2, C * D])
        XB = sb("XB", [P, 2, C * D])
        HH = sb("HH", [P, 2, C * D2])
        R = sb("R", [P, 2, C * D2])
        O = sb("O", [P, 2, C * D2])
        PG = sb("PG", [P, 2, PC * D])
        AT = sb("AT", [P, 2, 512])
        SX = sb("SX", [P, 2, 1024])
        XC = sb("XC", [P, C * D])
        SQ = sb("SQ", [P, C * D])
        IW = sb("IW", [P, 2, C], I32)
        st = sb("st", [P, 4, C])
        fw = sb("fw", [P, 2, 6, HCOLS])
        info = XC[:, 0:LOB * HI * 2].rearrange("p (l h c) -> p l h c", l=LOB, c=2)
        ident = sb("ident", [P, P])
        iota_h = sb("iota_h", [P, HI + 1], F16)
        relc = sb("relc", [P, RELS // 2])
        ones = sb("ones", [1, P])
        zeroh = sb("zeroh", [P, 512], F16)
        epsc = sb("epsc", [P, 1])
        W0 = sb("W0", [P, RELS // 2, D])
        WD = sb("WD", [P, 3, D])
        WS = sb("WS", [P, 3, D2])
        W12 = sb("W12", [P, D])
        WG1 = sb("WG1", [P, 2 * D2])
        WG2 = sb("WG2", [P, D2])
        BS = sb("BS", [1, 3, D2])
        BG2 = sb("BG2", [1, D2])
        ATTD = sb("ATTD", [P, HEADS])
        bl1b = sb("bl1b", [P, D2])
        lastb = sb("lastb", [P, D])
        blc = sb("blc", [P, 2])
        bsc = sb("bsc", [P, 4])
        attb2 = sb("attb2", [P, D])
        bias1c = sb("bias1c", [P, 1])
        bias2b = sb("bias2b", [P, D])
        CARRY = sb("CARRY", [P, P])
        cols = sb("cols", [P, 32])
        colsi = sb("colsi", [P, 8], I32)
        rowz = sb("rowz", [HEADS, 8, P])
        tz = sb("tz", [P, 8, HEADS])
        VB = sb("VB", [P, D])

        PS = ctx.enter_context(nc.psum_tensor("PS", [P, 8, 512], F32))

        def sem(name):
            return ctx.enter_context(nc.semaphore(name))

        bar = sem("phase_ended")
        chv, cha, chp = sem("dve_step"), sem("act_step"), sem("pool_step")
        s_fill, s_const = sem("fills_made"), sem("constants_made")
        s_in, s_w = sem("indices_loaded"), sem("weights_loaded")
        s_line, s_shift = sem("dst_line_stored"), sem("shifted_dst_loaded")
        s_keys = sem("index_columns_made")
        s_order = sem("edges_in_order")
        s_xn = [sem(f"node_rows_loaded{j}") for j in range(4)]
        XN = [HH[0:NP_, j // 2, j % 2 * C * D:j % 2 * C * D + NC * D] for j in range(4)]
        s_asked, s_moved = sem("sort_asked_of_pool"), sem("sort_rows_moved")
        s_move, s_place = sem("sort_dma_done"), [sem("records_placed0"), sem("records_placed1")]

        BITS = PAD.bit_length()
        SETUP_ASKS, PASS_ASKS = 3, 2
        g_flat, x_flat = (t.rearrange("p b n -> p (b n)") for t in (G[:], XB[:]))
        record = g_flat[:, 0:4 * TILES].bitcast(I32)
        fields_of = record.rearrange("p (t k) -> p k t", k=4)
        one, zeros, place, as_int = (g_flat[:, (4 + k) * TILES:(5 + k) * TILES] for k in range(4))
        number = x_flat[:, 0:TILES]
        all_sums, before_me, masked = (x_flat[:, TILES + k * P:TILES + (k + 1) * P] for k in range(3))
        few = x_flat[:, TILES + 3 * P:TILES + 3 * P + 8]
        w_record = x_flat[:, TILES + 4 * P:TILES + 4 * P + 4 * C].bitcast(I32)
        w_place = x_flat[:, TILES + 5 * P:TILES + 5 * P + C].bitcast(I32)
        places = place.bitcast(I32)
        s_cols = sem("partition_columns_made")
        s_trans = sem("setup_products_made")
        s_hot, s_binned, s_bins, s_info = sem("one_hots_made"), sem("one_hots_used"), sem("bins_made"), sem("node_info_stored")
        s_pg, s_pst, s_infog = [sem("x_rows_gathered0"), sem("x_rows_gathered1")], [sem("x_rows_stored0"), sem("x_rows_stored1")], sem("info_gathered")
        s_infoc = sem("info_copied")
        s_xc, s_sq, s_var, s_std = sem("ln_centred"), sem("ln_squared"), sem("ln_variance"), sem("ln_deviation")

        s_ld, s_st = [sem("loaded0"), sem("loaded1")], [sem("stored0"), sem("stored1")]
        s_turned, s_copied = sem("groups_transposed"), sem("transposed_copied")
        s_mult, s_out = sem("groups_multiplied"), sem("products_copied")
        s_ready, s_done = sem("chunk_ready"), sem("chunk_done")
        s_carry = sem("carry_multiplied")
        s_ldg = [sem("defaults_loaded0"), sem("defaults_loaded1")]
        s_g = [sem("gathered0"), sem("gathered1")]
        s_scan = sem("chunk_scanned")
        s_patch, s_patched = sem("patch_rows_gathered"), sem("patch_rows_scattered")
        s_prep, s_lone = sem("prep_step"), sem("lone_xl2_stored")
        s_exp, s_elu = sem("exponentials_made"), sem("elu_made")
        s_sums, s_leaky, s_scored = sem("score_sums_copied"), sem("leaky_made"), sem("groups_scored")
        s_sm = sem("softmax_step")
        s_last = sem("last_tails_known")
        s_scan2 = sem("dst_rows_spread")
        s_tot = [sem("totals_stored0"), sem("totals_stored1")]
        s_left = sem("left_halves_copied")
        s_rows = [sem("second_operands_stored0"), sem("second_operands_stored1")]
        SM_STEPS = 17
        s_sc = [sem("output_rows_scattered0"), sem("output_rows_scattered1")]
        s_turnedh = sem("turned_rows_copied")
        s_spread, s_mask = sem("rows_and_types_turned"), sem("masks_made")
        s_mmult, s_mout = sem("messages_multiplied"), sem("messages_copied")
        s_lmade, s_lput = sem("lone_units_made"), sem("lone_units_copied")

        def lone_units(groups, backs):
            stages = [("turn", 0, 0)] + [("step", k, k + 1) for k in range(3)] + [("back", k, k + 2) for k in backs]
            return [(stage, k, v - lag) for v in range(groups + 4) for stage, k, lag in stages if 0 <= v - lag < groups]

        def made_from(unit):
            stage, k, g = unit
            return {"step": ("step", k - 1, g) if k else ("turn", 0, g), "back": ("step", k, g)}[stage]

        SRC_UNITS, NODE_UNITS = lone_units(GROUPS, range(3)), lone_units(NGROUPS, [2])
        SRC_RING, NODE_RING = 2, 5
        CREDIT = 5
        PAIRS = C // 2
        SRC_AT = [O[:, k, C * D:C * D + 1024] for k in range(2)]
        NODE_AT = [SX[:, k, :] for k in range(2)]
        MASKED = [SX[:].rearrange("p b n -> p (b n)"), EE[:, 6:, :].rearrange("p k t -> p (k t)")[:, 0:2048]]
        TY = [tmp[:, b * C:(b + 1) * C] for b in range(2)]

        counts, before = {}, {}

        def plan(phase, **adds):
            for name, n in adds.items():
                before[phase, name] = counts.get(name, 0)
                counts[name] = counts.get(name, 0) + n

        plan("source", ld=TURNS * 16, st=5 * TURNS * 16, ln=2 * CHUNKS, lone=len(SRC_UNITS) * CHUNKS, ready=CHUNKS, done=CHUNKS, carry=1)
        plan("dest", ld=2 * TURNS * 16, st=2 * TURNS * 16, ln=CHUNKS, done=CHUNKS)
        plan("nodes", st=NCHUNKS // 2 * 16, ln=NCHUNKS, lone=len(NODE_UNITS) * NCHUNKS, ready=NCHUNKS, done=NCHUNKS)
        plan("prep", patch=16, carry=1)
        LAYERS = [f"layer{k}" for k in range(4)]
        for k, layer in enumerate(LAYERS):
            normed = k >= 2
            plan(layer, ldg=TURNS * 16, ld=(1 + normed) * TURNS * 16, st=(1 + normed) * TURNS * 16, tot=TURNS * 16, gath=TURNS * 16 * C,
                 scan=CHUNKS, ready=CHUNKS + 1, group=GROUPS * CHUNKS + 1, done=(CHUNKS + 1) * normed, ln=normed * (CHUNKS + 1), carry=1,
                 patch=(2 + normed) * 16, patched=(1 + normed) * 16)
        plan("att1", ldg=TURNS * 16, ld=TURNS * 16, st=TURNS * 16, gath=TURNS * 16 * C, ready=CHUNKS, group=GROUPS * CHUNKS, patch=16)
        plan("sum1", ld=TURNS * 16, st=TURNS * 16, scan=CHUNKS, ready=CHUNKS + 1, group=GROUPS * CHUNKS + 1, carry=1,
             patch=16, patched=32)
        plan("att2", ldg=TURNS * 16, ld=TURNS * 16, st=TURNS * 16, gath=TURNS * 16 * C, done=CHUNKS, patch=16)
        plan("sum2", ld=2 * TURNS * 16, st=TURNS * 16, scan=CHUNKS, ready=CHUNKS, carry=1, patch=32, patched=16)
        BAR = {name: n for n, name in enumerate(["setup", "bins", "source", "dest", "nodes", "prep"])}
        for name in LAYERS:
            BAR[name] = len(BAR)
            BAR[name + " patch"] = len(BAR)
        for name in ("att1", "soft1", "sum1", "sum1 patch", "att2", "soft2", "sum2", "sum2 patch"):
            BAR[name] = len(BAR)
        AHEAD = 2

        XL = [t.rearrange("p b n -> p (b n)") for t in (G[:], XB[:])]

        def chunk(t, c, width):
            return t[:, bass.ds(c * width, width)]

        def over(ap, n):
            return ap.unsqueeze(2).broadcast_to([ap.shape[0], ap.shape[1], n])

        def cut(ap, n=D):
            return ap.rearrange("p (m n) -> p m n", n=n)

        def paired(eng, turns, body, start=0):
            with eng.Fori(start, turns) as it:
                for b in range(2):
                    body(2 * it + b, it, b)

        class Barrier:

            def __init__(self, eng):
                self.eng, self.n = eng, 0

            def __call__(self):
                self.n += 1
                self.eng.drain().then_inc(bar, 1)
                self.eng.wait_ge(bar, 4 * self.n)

        def phases_over(eng, n):
            eng.wait_ge(bar, 4 * n)

        block = ctx.enter_context(nc.Block())

        @block.sync
        def _(sp):
            barrier = Barrier(sp)
            FULL = P - 1
            REST = E - FULL * TILES
            sp.wait_ge(s_fill, 6)
            for to, of in ((dsti, dst), (srci, src), (tmp[:].bitcast(I32), etype)):
                sp.dma_start(to[0:FULL, :], of[0:FULL * TILES].rearrange("(p t) -> p t", t=TILES)).then_inc(s_in, 16)
                sp.dma_start(to[FULL:P, 0:REST], of[FULL * TILES:E].rearrange("(p t) -> p t", p=1)).then_inc(s_in, 16)
            loads = [(W0[r * D:(r + 1) * D], w0.rearrange("(j r) k o -> r k j o", r=2)[r]) for r in range(2)]
            loads += [(WD[0:D], wl.rearrange("l k o -> k l o")), (WD[D:P], wr.rearrange("l k o -> k l o"))]
            loads += [(WS[r * D:(r + 1) * D, :, r * D:(r + 1) * D], wr.rearrange("l k o -> k l o")) for r in range(2)]
            loads += [(W12[0:D], w1), (W12[D:P], w2)]
            loads += [(SQ[:, 0:D], gwl1), (SQ[:, D:D2], gwr1), (SQ[0:D, D2:2 * D2], gwl2), (SQ[D:P, D2:2 * D2], gwr2)]
            loads += [(BS[:, :, r * D:(r + 1) * D], wb.unsqueeze(0)) for r in range(2)]
            loads += [(BG2[:, 0:D], gbl2.unsqueeze(0)), (BG2[:, D:], gbr2.unsqueeze(0))]
            loads += [(attb2[:], gatt2.rearrange("h c -> (h c)").partition_broadcast(P)),
                      (bias2b[:], gbias2.partition_broadcast(P)), (bias1c[:], gbias1.unsqueeze(1)),
                      (lastb[:], wb[2].partition_broadcast(P)), (bl1b[:], gbl1.partition_broadcast(P)), (blc[:, 0:1], gbl1.unsqueeze(1)), (blc[:, 1:2], gbr1.unsqueeze(1))]
            loads += [(ATTD[h * (D2 // HEADS):(h + 1) * (D2 // HEADS), h:h + 1], gatt1[h].unsqueeze(1)) for h in range(HEADS)]
            loads += [(bsc[r * D:(r + 1) * D, k:k + 1], wb[k].unsqueeze(1)) for r in range(2) for k in range(3)]
            loads += [(bsc[r * D:(r + 1) * D, 3:4], gbias2.unsqueeze(1)) for r in range(2)]
            assert len(loads) == WEIGHT_LOADS
            for to, of in loads:
                sp.dma_start(to, of).then_inc(s_w, 16)
            sp.wait_ge(s_order, 1)
            sp.dma_start(dst_line[1:ROWS + 1, :].rearrange("(p t) o -> p (t o)", t=TILES), dsti[:]).then_inc(s_line, 16)
            sp.dma_start(dst_line[0:1, :], colsi[0:1, NEG:NEG + 1]).then_inc(s_line, 16)
            sp.dma_start(dst_line[ROWS + 1:ROWS + 2, :], colsi[0:1, NEG:NEG + 1]).then_inc(s_line, 16)
            sp.wait_ge(s_line, 48)
            for to, at in ((Ea[:, 0, :], 0), (Ea[:, 1, :], 2)):
                sp.dma_start(to.bitcast(I32), dst_line[at:at + ROWS, :].rearrange("(p t) o -> p (t o)", t=TILES)
                             ).then_inc(s_shift, 16)
            barrier()
            sp.wait_ge(s_bins, 1)
            sp.dma_start(node_info.rearrange("(p r) c -> p (r c)", p=P), info.rearrange("p l h c -> p (l h c)")
                         ).then_inc(s_info, 16)
            sp.wait_ge(s_info, 16)
            barrier()

            def streams(phase, chunks, loads, stores, begin=None):
                def load(i, it, b):
                    if begin:
                        begin(i, it, b)
                    for to, of in loads(i, b):
                        sp.dma_start(to, of).then_inc(s_ld[b], 16)

                def store(i, it, b):
                    sp.wait_ge(s_done, before[phase, "done"] + 1 + i)
                    for to, of in stores(i, b):
                        sp.dma_start(to, of).then_inc(s_st[b], 16)
                    sp.wait_ge(s_st[b], before[phase, "st"] + 16 * len(stores(0, 0)) * (it + 1))

                for b in range(2):
                    load(b, 0, b)

                def turn(i, it, b):
                    store(i, it, b)
                    load(i + 2, it + 1, b)

                paired(sp, chunks // 2 - 1, turn)
                for b in range(2):
                    store(chunks - 2 + b, chunks // 2 - 1, b)

            def x_rows_there(which):
                def wait(i, it, b):
                    for k in range(2):
                        sp.wait_ge(s_pst[k], 16 * (which * (PCHUNKS // 2) + 1 + i))
                return wait

            CD = C * D
            streams("source", CHUNKS, lambda i, b: [(XB[:, b, :], chunk(xsrc, i, CD))],
                    lambda i, b: [(chunk(lone[0], i, CD), G[:, b, :]), (chunk(lone[1], i, CD), HH[:, b, 0:CD]),
                                  (chunk(lone[2], i, CD), HH[:, b, CD:]), (chunk(lone[3], i, CD), O[:, b, 0:CD]),
                                  (chunk(total[0], i, CD), R[:, b, CD:])], x_rows_there(0))
            barrier()
            streams("dest", CHUNKS, lambda i, b: [(XB[:, b, :], chunk(xdst, i, CD)), (R[:, b, 0:CD], chunk(total[0], i, CD))],
                    lambda i, b: [(chunk(resid[0], i, CD), XB[:, b, :]), (chunk(table[0], i, CD), G[:, b, :])], x_rows_there(1))
            barrier()
            x_nodes, out_nodes = (t.rearrange("(p t) f -> p (t f)", p=NP_) for t in (x, out))

            def load_nodes(i, j):
                sp.dma_start(XN[j], chunk(x_nodes, i, NC * D)).then_inc(s_xn[j], 16)

            def store_nodes(i, j, more=True):
                sp.wait_ge(s_done, before["nodes", "done"] + 1 + i)
                if more:
                    load_nodes(i + 4, j)
                sp.dma_start(chunk(out_nodes, i, NC * D), R[0:NP_, j % 2, 0:NC * D]).then_inc(s_st[j % 2], 16)

            for j in range(4):
                load_nodes(j, j)
            with sp.Fori(0, NCHUNKS // 4 - 1) as it:
                for j in range(4):
                    store_nodes(4 * it + j, j)
            for j in range(4):
                store_nodes(NCHUNKS - 4 + j, j, more=False)
            for b in range(2):
                sp.wait_ge(s_st[b], before["nodes", "st"] + 16 * (NCHUNKS // 2))
            barrier()
            sp.wait_ge(s_prep, 4)
            sp.dma_start(lone_xl2, XC[:]).then_inc(s_lone, 16)
            sp.wait_ge(s_lone, 16)
            barrier()

            def layer_streams(phase, early, late, stores, early_free, finished, c_of=lambda i: i, totals=None):
                def load_early(i, it, b):
                    for to, of in early(c_of(i), b):
                        sp.dma_start(to, of).then_inc(s_ldg[b], 16)

                def load_late(i, it, b):
                    for to, of in late(c_of(i), b):
                        sp.dma_start(to, of).then_inc(s_ld[b], 16)

                def store(i, it, b):
                    finished(i, b)
                    for to, of in stores(c_of(i), b):
                        sp.dma_start(to, of).then_inc(s_st[b], 16)
                    sp.wait_ge(s_st[b], before[phase, "st"] + 16 * len(stores(0, 0)) * (it + 1))

                for b in range(2):
                    load_early(b, 0, b)
                    load_late(b, 0, b)

                def turn(i, it, b):
                    store(i, it, b)
                    load_early(i + 2, it + 1, b)
                    load_late(i + 2, it + 1, b)

                def early_turn(i, b, last_it):
                    early_free(i)
                    load_early(i + 2, None, b)
                    store_totals(i, b)
                    store(i - 1, last_it, 1 - b)
                    load_late(i + 1, None, 1 - b)

                def store_totals(i, b):
                    if totals is not None:
                        sp.dma_start(chunk(totals, c_of(i), CD), R[:, b, 0:CD]).then_inc(s_tot[b], 16)

                if early_free:
                    early_free(0)
                    load_early(2, 1, 0)
                    store_totals(0, 0)
                    with sp.Fori(0, TURNS - 2) as it:
                        early_turn(2 * it + 1, 1, it)
                        early_turn(2 * it + 2, 0, it)
                    early_turn(CHUNKS - 3, 1, TURNS - 2)
                    store(CHUNKS - 3, TURNS - 2, 1)
                    load_late(CHUNKS - 1, TURNS - 1, 1)
                else:
                    paired(sp, TURNS - 1, turn)
                for b in range(2):
                    if totals is not None:
                        early_free(CHUNKS - 2 + b)
                        store_totals(CHUNKS - 2 + b, b)
                        sp.wait_ge(s_tot[b], before[phase, "tot"] + 16 * (TURNS + 1))
                    store(CHUNKS - 2 + b, TURNS - 1, b)

            def products_out(phase):
                def wait(i, b):
                    sp.wait_ge(s_out, before[phase, "group"] + AHEAD + GROUPS * (i + 1))
                return wait

            def chunk_done(phase):
                def wait(i, b):
                    sp.wait_ge(s_done, before[phase, "done"] + 1 + i)
                return wait

            def patched(phase, n):
                sp.wait_ge(s_patched, before[phase, "patched"] + 16 * n)

            for k, layer in enumerate(LAYERS):
                normed = k >= 2
                right = lambda b: cut(HH[:, b, :], D2)[:, :, D:]
                layer_streams(
                    layer, lambda c, b: [(G[:, b, :], chunk(lone[k], c, CD))],
                    lambda c, b: [(right(b), cut(chunk(table[k], c, CD)))] + [(XB[:, b, :], chunk(resid[k - 2], c, CD))] * normed,
                    lambda c, b: [(chunk(table[k + 1], c, CD), O[:, b, 0:CD])]
                    + [(chunk(resid[k - 1], c, CD), XB[:, b, :])] * normed,
                    lambda i: sp.wait_ge(s_scan, before[layer, "scan"] + 1 + i),
                    chunk_done(layer) if normed else products_out(layer), totals=total[k + 1])
                barrier()
                patched(layer, 1 + normed)
                barrier()
            def att1_states(i, b):
                sp.dma_start(XB[:, b, :], chunk(table[4], i * (-1) + (CHUNKS - 1), CD)).then_inc(s_ld[b], 16)

            def att1_defaults(i, b):
                sp.dma_start(G[:, b, :], chunk(lone[3], i * (-1) + (CHUNKS - 1), CD)).then_inc(s_ldg[b], 16)

            def att1_turn(i, it, b, more=True):
                if more:
                    sp.wait_ge(s_ready, before["att1", "ready"] + 1 + i)
                    att1_states(i + 2, b)
                    sp.wait_ge(s_left, 1 + i)
                    att1_defaults(i + 2, b)
                products_out("att1")(i, b)
                sp.dma_start(chunk(xl1, i * (-1) + (CHUNKS - 1), 2 * CD), O[:, b, :]).then_inc(s_st[b], 16)

            for b in range(2):
                att1_states(b, b)
                att1_defaults(b, b)
            paired(sp, TURNS - 1, att1_turn)
            for b in range(2):
                att1_turn(CHUNKS - 2 + b, None, b, more=False)
                sp.wait_ge(s_st[b], before["att1", "st"] + 16 * TURNS)
            barrier()
            barrier()
            def load_sums(i, b):
                sp.dma_start(XL[b], chunk(xl1, i, 2 * CD)).then_inc(s_ld[b], 16)

            def sums(i, it, b, more=True):
                sp.wait_ge(s_scan, before["sum1", "scan"] + 1 + i)
                sp.dma_start(chunk(total_g1, i, 2 * CD), R[:, b, :]).then_inc(s_st[b], 16)
                sp.wait_ge(s_st[b], before["sum1", "st"] + 16 * (it + 1))
                if more:
                    load_sums(i + 2, b)
                products_out("sum1")(i, b)
                sp.dma_start(chunk(table_l2, i, CD), O[:, b, 0:CD]).then_inc(s_rows[b], 16)
                sp.dma_start(chunk(table_r2, i, CD), O[:, b, CD:]).then_inc(s_rows[b], 16)

            for b in range(2):
                load_sums(b, b)
            paired(sp, TURNS - 1, sums)
            for b in range(2):
                sums(CHUNKS - 2 + b, TURNS - 1, b, more=False)
                sp.wait_ge(s_rows[b], 32 * (TURNS + 1))
            barrier()
            patched("sum1", 2)
            barrier()
            layer_streams(
                "att2", lambda c, b: [(G[:, b, :], lone_xl2)],
                lambda c, b: [(XB[:, b, :], chunk(table_r2, c, CD))],
                lambda c, b: [(chunk(xl2, c, CD), G[:, b, :])],
                None, chunk_done("att2"), lambda i: (CHUNKS - 1) - i if isinstance(i, int) else i * (-1) + (CHUNKS - 1))
            barrier()
            barrier()

            def scattered(i, b):
                sp.wait_ge(s_ready, before["sum2", "ready"] + 1 + i)
                sp.wait_ge(s_sc[b], 16 * C * ((i - b) // 2 + 1) if isinstance(i, int) else (i - b) * (8 * C) + 16 * C)

            layer_streams(
                "sum2", lambda c, b: [], lambda c, b: [(G[:, b, :], chunk(xl2, c, CD)), (XB[:, b, :], chunk(resid[2], c, CD))],
                lambda c, b: [(chunk(total_g2, c, CD), R[:, b, 0:CD])], None, scattered)
            barrier()
            patched("sum2", 1)
            barrier()

        @block.gpsimd
        def _(pool):
            step = Chain(pool, chp)
            pool.memset(dsti[:], PAD).then_inc(s_fill, 1)
            pool.memset(srci[:], PAD).then_inc(s_fill, 1)
            pool.memset(tmp[:].bitcast(I32), 0).then_inc(s_fill, 1)
            pool.memset(colsi[:], -1).then_inc(s_fill, 1)
            pool.memset(WS[:], 0.0).then_inc(s_fill, 1)
            pool.memset(ATTD[:], 0.0).then_inc(s_fill, 1)
            step(pool.memset(ident[:], 0.0))
            pool.affine_select(out=ident[:], in_=ident[:], compare_op=ALU.not_equal, fill=1.0, base=0,
                               pattern=[[-1, P]], channel_multiplier=1).then_inc(s_const, 1)
            step(pool.memset(CARRY[:], 1.0))
            pool.affine_select(out=CARRY[:], in_=CARRY[:], compare_op=ALU.is_gt, fill=0.0, base=0,
                               pattern=[[1, P]], channel_multiplier=-1).then_inc(s_const, 1)
            pool.iota(XC[:, 0:HI + 1].bitcast(I32), pattern=[[1, HI + 1]], base=0, channel_multiplier=0).then_inc(s_const, 1)
            pool.iota(Ea[:, 2, :].bitcast(I32), pattern=[[1, TILES]], base=0, channel_multiplier=TILES).then_inc(s_const, 1)
            pool.memset(PG[:], 0.0).then_inc(s_const, 1)

            def gather(to, table_, idx, bound, signal):
                return pool.indirect_dma_start(to, None, table_, bass.IndirectOffsetOnAxis(ap=idx, axis=0),
                                               bounds_check=bound, oob_is_err=False).then_inc(signal, 16)

            moved = 0

            def move(to, of):
                nonlocal moved
                moved += 1
                pool.dma_start(to, of).then_inc(s_move, 16)
                pool.wait_ge(s_move, 16 * moved)

            pool.wait_ge(s_asked, 1)
            move(sort_line, few[:, 0:1])
            move(few[1:P, 1:2], sort_line[0:P - 1])
            pool.drain().then_inc(s_moved, 1)
            pool.wait_ge(s_asked, 2)
            move(sort_line, few[:, 0:1])
            move(all_sums[0:1, :], sort_line.rearrange("p o -> o p"))
            pool.drain().then_inc(s_moved, 1)
            pool.wait_ge(s_asked, 3)
            disorder = pool.value_load(few[0:1, 3:4].bitcast(I32), min_val=0, max_val=1)
            step.reset()
            with pool.If(disorder > 0):
                step(pool.iota(as_int.bitcast(I32), pattern=[[1, TILES]], base=0, channel_multiplier=TILES))
                step(pool.memset(masked, 1.0))
                step(pool.affine_select(out=before_me, in_=masked, compare_op=ALU.is_gt, fill=0.0, base=0,
                                        pattern=[[-1, P]], channel_multiplier=1))
                pool.nop().then_inc(s_moved, 1)
                with pool.Fori(0, BITS) as bit:
                    step.reset()

                    def settle():
                        step(pool.tensor_tensor(few[:, 7:8], few[:, 7:8], few[:, 7:8], ALU.subtract))

                    def moved_in_pass(n):
                        pool.wait_ge(s_move, bit * (3 * 16) + 16 * (moved + n))
                        settle()

                    pool.wait_ge(s_asked, bit * PASS_ASKS + (SETUP_ASKS + 1))
                    settle()
                    pool.dma_start(sort_line, few[:, 0:1]).then_inc(s_move, 16)
                    moved_in_pass(1)
                    pool.dma_start(all_sums, sort_line.rearrange("p o -> (p o)").partition_broadcast(P)).then_inc(s_move, 16)
                    moved_in_pass(2)
                    pool.drain().then_inc(s_moved, 1)
                    pool.wait_ge(s_asked, bit * PASS_ASKS + (SETUP_ASKS + 2))
                    settle()
                    with pool.Fori(0, TURNS) as it:
                        for b in range(2):
                            step.reset()
                            w = 2 * it + b
                            step(pool.tensor_copy(w_record, record[:, bass.ds(w * (4 * C), 4 * C)]))
                            step(pool.tensor_copy(w_place, places[:, bass.ds(w * C, C)]))
                            for j in range(C):
                                pool.indirect_dma_start(sort_rows, bass.IndirectOffsetOnAxis(ap=w_place[:, j:j + 1], axis=0),
                                                        w_record[:, 4 * j:4 * j + 4], None, bounds_check=ROWS - 1,
                                                        oob_is_err=False).then_inc(s_place[b], 16)
                            pool.wait_ge(s_place[b], bit * (TURNS * 16 * C) + it * (16 * C) + 16 * C)
                            settle()
                    pool.dma_start(record, sort_rows.rearrange("(p t) k -> p (t k)", t=TILES)).then_inc(s_move, 16)
                    moved_in_pass(3)
                    pool.drain().then_inc(s_moved, 1)
                step.reset()

            pool.wait_ge(s_keys, 1)
            step(pool.memset(IW[:], 0))
            for which, (idx, to) in enumerate(((srci, xsrc), (dsti, xdst))):
                def turn(it, b, first):
                    step.reset()
                    if not first:
                        pool.wait_ge(s_pst[b], 16 * (it + which * (PCHUNKS // 2)))
                    step(pool.tensor_copy(IW[:, b, 0:PC], idx[:, bass.ds((2 * it + b) * PC, PC)]))
                    for j in range(PC):
                        gather(PG[:, b, j * D:(j + 1) * D], x, IW[:, b, j:j + 1], N - 1, s_pg[b])
                    pool.wait_ge(s_pg[b], 16 * PC * (it + 1 + which * (PCHUNKS // 2)))
                    pool.wait_ge(chp, 1)
                    pool.dma_start(chunk(to, 2 * it + b, PC * D), PG[:, b, :]).then_inc(s_pst[b], 16)
                if which == 0:
                    for b in range(2):
                        turn(0, b, True)
                with pool.Fori(1 - which, PCHUNKS // 2) as it:
                    for b in range(2):
                        turn(it, b, False)
            for b in range(2):
                pool.wait_ge(s_pst[b], 16 * PCHUNKS)
            pool.wait_ge(s_info, 16)
            for which, idx in enumerate((srcq, dstq)):
                with pool.Fori(0, CHUNKS) as i:
                    step.reset()
                    step(pool.tensor_copy(IW[:, 0, :], idx[:, bass.ds(i * C, C)]))
                    for j in range(C):
                        gather(PG[:, 0, 2 * j:2 * j + 2], node_info, IW[:, 0, j:j + 1], P * LOB * HI - 1, s_infog)
                    pool.wait_ge(s_infog, 16 * C * (i + 1 + which * CHUNKS))
                    pool.wait_ge(chp, 1)
                    step(pool.tensor_copy(EE[:, 4 * which:4 * which + 2, bass.ds(i * C, C)].rearrange("p c t -> p t c"),
                                          PG[:, 0, 0:2 * C].rearrange("p (t c) -> p t c", c=2)))
                pool.wait_ge(chp, 2)
            gather(PG[:, 0, 0:2], node_info, colsi[:, IX_LASTQ:IX_LASTQ + 1], P * LOB * HI - 1, s_patch)
            pool.drain().then_inc(s_infoc, 1)

            def after(phase):
                pool.wait_ge(bar, 4 * BAR[phase])

            def gathers(phase, table_, to):
                def turn(i, it, b):
                    step.reset()
                    pool.wait_ge(s_ldg[b], before[phase, "ldg"] + 16 * (it + 1))
                    c = i if phase in LAYERS else i * (-1) + (CHUNKS - 1)
                    step(pool.tensor_copy(IW[:, b, :], srcq[:, bass.ds(c * C, C)]))
                    for j in range(C):
                        gather(to(b, j), table_, IW[:, b, j:j + 1], ROWS - 1, s_g[b])
                paired(pool, TURNS, turn)

            def scatter(of, table_, idx, bound, signal):
                return pool.indirect_dma_start(table_, bass.IndirectOffsetOnAxis(ap=idx, axis=0), of, None,
                                               bounds_check=bound, oob_is_err=False).then_inc(signal, 16)

            at_tail, to_tail, last_tail = colsi[:, IX_FTG:IX_FTG + 1], colsi[:, IX_FT:IX_FT + 1], colsi[:, IX_LAST:IX_LAST + 1]

            for k, layer in enumerate(LAYERS):
                normed = k >= 2
                after(layer)
                gathers(layer, by_row(table[k]), lambda b, j: G[:, b, j * D:(j + 1) * D])
                after(layer + " patch")
                gather(R[:, 0, 0:D], by_row(total[k + 1]), at_tail, ROWS - 1, s_patch)
                gather(HH[:, 0, D:D2], by_row(table[k]), at_tail, ROWS - 1, s_patch)
                if normed:
                    gather(XB[:, 0, 0:D], by_row(resid[k - 2]), at_tail, ROWS - 1, s_patch)
                    pool.wait_ge(s_done, before[layer, "done"] + CHUNKS + 1)
                else:
                    pool.wait_ge(s_out, before[layer, "group"] + AHEAD + GROUPS * CHUNKS + 1)
                scatter(O[:, 0, 0:D], by_row(table[k + 1]), to_tail, ROWS - 1, s_patched)
                if normed:
                    scatter(XB[:, 0, 0:D], by_row(resid[k - 1]), to_tail, ROWS - 1, s_patched)
            after("att1")
            gather(VB[:], by_row(table[4]), last_tail, ROWS - 1, s_patch)
            gathers("att1", by_row(table[4]), lambda b, j: G[:, b, j * D:(j + 1) * D])
            after("sum1 patch")
            gather(R[:, 0, 0:D2], by_row(total_g1, D2), at_tail, ROWS - 1, s_patch)
            pool.wait_ge(s_out, before["sum1", "group"] + AHEAD + GROUPS * CHUNKS + 1)
            scatter(O[:, 0, 0:D], by_row(table_l2), to_tail, ROWS - 1, s_patched)
            scatter(O[:, 0, C * D:C * D + D], by_row(table_r2), to_tail, ROWS - 1, s_patched)
            after("att2")
            gather(VB[:], by_row(table_r2), last_tail, ROWS - 1, s_patch)
            gathers("att2", by_row(table_l2), lambda b, j: G[:, b, j * D:(j + 1) * D])
            after("sum2")

            def output(i, it, b):
                step.reset()
                pool.wait_ge(s_ready, before["sum2", "ready"] + 1 + i)
                step(pool.tensor_copy(IW[:, b, :], dstq[:, bass.ds(i * C, C)]))
                for j in range(C):
                    scatter(O[:, b, j * D:(j + 1) * D], out, IW[:, b, j:j + 1], N - 1, s_sc[b])

            paired(pool, TURNS, output)
            after("sum2 patch")
            gather(R[:, 0, 0:D], by_row(total_g2), at_tail, ROWS - 1, s_patch)
            gather(XB[:, 0, 0:D], by_row(resid[2]), at_tail, ROWS - 1, s_patch)
            pool.wait_ge(s_sm, SM_STEPS)
            scatter(O[:, 0, 0:D], out, colsi[:, IX_OUT:IX_OUT + 1], N - 1, s_patched)
            pool.wait_ge(s_patched, counts["patched"])

        @block.vector
        def _(dve):
            step = Chain(dve, chv)
            barrier = Barrier(dve)
            cast, tt, ts = dve.tensor_copy, dve.tensor_tensor, dve.tensor_scalar

            def col(k):
                return cols[:, k:k + 1]

            def coli(k):
                return colsi[:, k:k + 1]

            step(dve.memset(zeroh[:], 0.0))
            step(dve.memset(ones[:], 1.0))
            step(dve.memset(epsc[:], EPS))
            step(dve.memset(HH[:], 0.0))
            step(dve.memset(R[:], 0.0))
            dve.wait_ge(s_const, 5)
            step(cast(iota_h[:], XC[:, 0:HI + 1].bitcast(I32)))
            step(cast(relc[:], XC[:, 0:RELS // 2].bitcast(I32)))
            step(ts(relc[0:D], relc[0:D], 2.0, None, ALU.mult))
            step(ts(relc[D:P], relc[D:P], 2.0, 1.0, ALU.mult, ALU.add))
            dve.wait_ge(s_in, 16 * 6)
            asked = 0

            def ask(ins):
                nonlocal asked
                asked += 1
                ins.then_inc(s_asked, 1)

            step(cast(number, dsti[:]))
            step(dve.memset(few[:], -1.0))
            ask(cast(few[:, 0:1], number[:, TILES - 1:TILES]))
            dve.wait_ge(s_moved, 1)
            step(tt(one[:, 1:], number[:, 0:TILES - 1], number[:, 1:], ALU.is_gt))
            step(tt(one[:, 0:1], few[:, 1:2], number[:, 0:1], ALU.is_gt))
            ask(dve.tensor_reduce(few[:, 0:1], one, AX_X, ALU.max))
            dve.wait_ge(s_moved, 2)
            step(dve.tensor_reduce(few[0:1, 2:3], all_sums[0:1, :], AX_X, ALU.max))
            ask(cast(few[0:1, 3:4].bitcast(I32), few[0:1, 2:3]))
            dve.wait_ge(s_asked, SETUP_ASKS)
            disorder = dve.value_load(few[0:1, 3:4].bitcast(I32), min_val=0, max_val=1)
            step.reset()
            with dve.If(disorder > 0):
                dve.wait_ge(s_moved, 3)
                step(cast(number, as_int.bitcast(I32)))
                for k, of in enumerate((dsti[:], dsti[:], srci[:], tmp[:].bitcast(I32))):
                    step(cast(fields_of[:, k, :], of))
                step(dve.memset(place, 1.0))
                with dve.Fori(0, BITS) as bit:
                    step.reset()
                    key = fields_of[:, 0, :]
                    step(ts(as_int.bitcast(I32), key, 1, None, ALU.bitwise_and))
                    step(cast(one, as_int.bitcast(I32)))
                    step(ts(key, key, 1, None, ALU.logical_shift_right))
                    step(ts(as_int, one, -1.0, 1.0, ALU.mult, ALU.add))
                    step(dve.memset(place, 1.0))
                    step(dve.tensor_tensor_scan(out=zeros, data0=place, data1=as_int, initial=0.0, op0=ALU.mult, op1=ALU.add))
                    cast(few[:, 0:1], zeros[:, TILES - 1:TILES]).then_inc(s_asked, 1)
                    dve.wait_ge(s_moved, bit * PASS_ASKS + 4)
                    step(dve.memset(few[:, 6:7], 0.0))
                    step(dve.tensor_reduce(few[:, 1:2], all_sums, AX_X, ALU.add))
                    step(tt(masked, all_sums, before_me, ALU.mult))
                    step(dve.tensor_reduce(few[:, 2:3], masked, AX_X, ALU.add))
                    step(ts(zeros, zeros, few[:, 2:3], None, ALU.add))
                    step(tt(as_int, number, zeros, ALU.subtract))
                    step(ts(as_int, as_int, few[:, 1:2], None, ALU.add))
                    step(ts(zeros, zeros, -1.0, None, ALU.add))
                    step(tt(as_int, as_int, zeros, ALU.subtract))
                    step(tt(as_int, as_int, one, ALU.mult))
                    step(tt(as_int, as_int, zeros, ALU.add))
                    cast(places, as_int).then_inc(s_asked, 1)
                    dve.wait_ge(s_moved, bit * PASS_ASKS + 5)
                    step(dve.memset(few[:, 6:7], 0.0))
                step.reset()
                for k, to in enumerate((dsti[:], srci[:], tmp[:].bitcast(I32))):
                    step(cast(to, fields_of[:, k + 1, :]))
                step.reset()
            dve.drain().then_inc(s_order, 1)
            step(cast(etf[:], tmp[:].bitcast(I32)))
            scr_i, scr_f = O[:, 0, 0:TILES].bitcast(I32), O[:, 0, TILES:2 * TILES]
            acc_f = O[:, 0, 2 * TILES:3 * TILES]
            fields = {}
            for k, (key, q) in enumerate(((srci, srcq), (dsti, dstq))):
                hi_f, lo_f = EE[:, 3 + 2 * k, :], EE[:, 4 + 2 * k, :]
                fields[k] = (hi_f, lo_f)
                step(ts(scr_i, key[:], 8, None, ALU.logical_shift_right))
                step(cast(hi_f, scr_i))
                step(ts(scr_i, key[:], 255, None, ALU.bitwise_and))
                step(cast(lo_f, scr_i))
                step(ts(scr_i, key[:], 127, None, ALU.bitwise_and))
                step(cast(scr_f, scr_i))
                step(dve.scalar_tensor_tensor(out=acc_f, in0=scr_f, scalar=float(LOB * HI), in1=hi_f, op0=ALU.mult, op1=ALU.add))
                step(ts(scr_i, key[:], 7, 1, ALU.logical_shift_right, ALU.bitwise_and))
                step(cast(scr_f, scr_i))
                step(dve.scalar_tensor_tensor(out=acc_f, in0=scr_f, scalar=float(HI), in1=acc_f, op0=ALU.mult, op1=ALU.add))
                step(cast(q[:], acc_f))
            step(ts(col(SCR), acc_f[:, TILES - 1:TILES], float(P * LOB * HI - 1), None, ALU.min))
            step(cast(coli(IX_LASTQ), col(SCR)))
            dve.nop().then_inc(s_keys, 1)
            dve.wait_ge(s_shift, 32)
            dst_f, prev_f, next_f = O[:, 0, 0:TILES], O[:, 0, TILES:2 * TILES], O[:, 0, 2 * TILES:3 * TILES]
            step(cast(dst_f, dsti[:]))
            step(cast(prev_f, Ea[:, 0, :].bitcast(I32)))
            step(cast(next_f, Ea[:, 1, :].bitcast(I32)))
            step(tt(same[:], dst_f, prev_f, ALU.is_equal))
            step(tt(tail[:], dst_f, next_f, ALU.not_equal))
            step(tt(rest[:], dst_f, next_f, ALU.is_equal))
            step(cast(col(JP), same[:, 0:1]))
            step(cast(col(JN), rest[:, TILES - 1:TILES]))
            step(dve.memset(same[:, 0:1], 0.0))
            step(cast(col(DF), dst_f[:, 0:1]))
            step(cast(col(DL), dst_f[:, TILES - 1:TILES]))
            step(tt(col(WH), col(DF), col(DL), ALU.is_equal))
            step(ts(first_seg[:], dst_f, col(DF), None, ALU.is_equal))
            step(ts(last_seg[:], dst_f, col(DL), None, ALU.is_equal))
            step(tt(first_tail[:], first_seg[:], tail[:], ALU.mult))
            rowid = O[:, 0, 3 * TILES:4 * TILES]
            prod = O[:, 0, 4 * TILES:5 * TILES]
            step(cast(rowid, Ea[:, 2, :].bitcast(I32)))

            def at_first_tail(out_col, values):
                step(tt(prod, values, first_tail[:], ALU.mult))
                step(dve.tensor_reduce(out_col, prod, AX_X, ALU.add))

            at_first_tail(col(FT_ROW), rowid)
            step(dve.tensor_reduce(col(FT_HAS), first_tail[:], AX_X, ALU.add))
            at_first_tail(col(FT_OUT), dst_f)
            step(cast(coli(IX_FTG), col(FT_ROW)))
            step(ts(col(MISS), col(FT_HAS), -FAR, FAR, ALU.mult, ALU.add))
            step(tt(col(FT_ROW), col(FT_ROW), col(MISS), ALU.add))
            step(cast(coli(IX_FT), col(FT_ROW)))
            step(tt(col(FT_OUT), col(FT_OUT), col(MISS), ALU.add))
            step(cast(coli(IX_OUT), col(FT_OUT)))
            for cap, pen, join in ((CAP_P, PEN_P, JP), (CAP_N, PEN_N, JN)):
                step(ts(col(cap), col(join), BIG, -BIG, ALU.mult, ALU.add))
                step(tt(col(pen), col(join), col(WH), ALU.mult))
                step(ts(col(pen), col(pen), BIG, -BIG, ALU.mult, ALU.add))
            step(ts(prod, rowid, 1.0, None, ALU.add))
            step(tt(prod, prod, tail[:], ALU.mult))
            step(cast(scr_i, prod))
            step(ts(prev_f.bitcast(I32), scr_i, 8, None, ALU.logical_shift_right))
            step(cast(EE[:, 7, :], prev_f.bitcast(I32)))
            step(ts(prev_f.bitcast(I32), scr_i, 255, None, ALU.bitwise_and))
            step(cast(EE[:, 8, :], prev_f.bitcast(I32)))
            dve.nop().then_inc(s_cols, 1)
            dve.wait_ge(s_trans, 1)
            step(ts(prod[:, 0:P], PS[:, 0, 0:P], col(DL), None, ALU.is_equal))
            step(tt(CARRY[:], CARRY[:], prod[:, 0:P], ALU.mult))
            dve.wait_ge(s_trans, 3)
            dve.wait_ge(s_w, 16 * WEIGHT_LOADS)
            step(cast(WG1[:, 0:D2], PS[:, 1, 0:D2]))
            step(cast(WG1[0:D, D2:], PS[0:D, 1, 0:D2]))
            step(dve.memset(WG1[D:P, D2:], 0.0))
            step(cast(WG2[:], PS[:, 1, D2:2 * D2]))
            step(tt(blc[:, 0:1], blc[:, 0:1], blc[:, 1:2], ALU.add))
            step(tt(bsc[:, 3:4], bsc[:, 3:4], bsc[:, 2:3], ALU.add))
            dve.wait_ge(s_trans, 7)
            step(cast(rowz[:, 0:4, :].rearrange("h k p -> h (k p)"), PS[0:HEADS, 2, 0:4 * P]))
            step(dve.memset(prod, 1.0))
            step(dve.tensor_tensor_scan(out=inv_in[:], data0=same[:], data1=prod, initial=0.0, op0=ALU.mult, op1=ALU.add))
            dve.nop().then_inc(s_keys, 1)
            dve.wait_ge(s_trans, 8)
            step(cast(col(CNT_C), PS[:, 3, 0:1]))
            step(dve.scalar_tensor_tensor(out=inv_in[:], in0=first_seg[:], scalar=col(CNT_C), in1=inv_in[:], op0=ALU.mult, op1=ALU.add))
            dve.nop().then_inc(s_keys, 1)
            dve.wait_ge(s_trans, 9)
            step(dve.reciprocal(rs_in[:], rs_in[:]))
            step(dve.reciprocal(inv_in[:], inv_in[:]))
            at_first_tail(col(INV_FT), inv_in[:])
            at_first_tail(col(RSIN_FT), rs_in[:])
            barrier()

            Rh = R[:, :, :].bitcast(F16)

            def hot(b):
                return Rh[:, b, 0:HCOLS * HSLOT].rearrange("p (k s) -> p k s", k=HCOLS)

            with dve.Fori(0, HTURNS) as it:
                for b in range(2):
                    step.reset()
                    dve.wait_ge(s_binned, 2 * it + b + 1)
                    step(cast(fw[:, b, :, :], EE[:, 3:9, bass.ds((2 * it + b) * HCOLS, HCOLS)]))
                    h1 = HI + 1
                    for k in range(HCOLS):
                        sc = [fw[:, b, f, k:k + 1] for f in range(6)]
                        o = hot(b)[:, k, :]
                        ts(o[:, 0:h1], iota_h[:], sc[0], None, ALU.is_equal)
                        ts(o[:, h1:2 * h1], iota_h[:], sc[2], sc[4], ALU.is_equal, ALU.mult)
                        ts(o[:, 2 * h1:3 * h1], iota_h[:], sc[2], sc[5], ALU.is_equal, ALU.mult)
                        ts(o[:, 3 * h1:3 * h1 + 256], iota_h[:, 0:256], sc[1], None, ALU.is_equal)
                        last = ts(o[:, 3 * h1 + 256:], iota_h[:, 0:256], sc[3], None, ALU.is_equal)
                    last.then_inc(s_hot, 1)
            dve.wait_ge(s_binned, 2 * HTURNS + 3)
            step.reset()
            for l in range(LOB):
                step(cast(info[:, l, :, 1], PS[:, l, 0:HI]))
                step(cast(info[:, l, :, 0], PS[:, LOB + l, 0:HI]))
                step(dve.scalar_tensor_tensor(out=info[:, l, :, 0], in0=info[:, l, :, 0], scalar=256.0,
                                              in1=PS[:, 2 * LOB + l, 0:HI], op0=ALU.mult, op1=ALU.add))
            dve.nop().then_inc(s_bins, 1)
            barrier()

            def norm(x_in, h_out, n, ln, parts=P):
                xc, sq = cut(XC[0:parts, 0:n * D]), cut(SQ[0:parts, 0:n * D])
                mean, var, dev, inv = (st[0:parts, k, 0:n] for k in range(4))
                step(dve.tensor_reduce(mean, cut(x_in), AX_X, ALU.add))
                step(ts(mean, mean, 1.0 / D, None, ALU.mult))
                tt(xc, cut(x_in), over(mean, D), ALU.subtract).then_inc(s_xc, 1)
                dve.wait_ge(s_sq, ln)
                dve.tensor_reduce(var, sq, AX_X, ALU.add).then_inc(s_var, 1)
                dve.wait_ge(s_std, ln)
                step(dve.reciprocal(inv, dev))
                return dve.scalar_tensor_tensor(out=cut(h_out), in0=xc, scalar=0.0, in1=over(inv, D), op0=ALU.max, op1=ALU.mult)

            def scans(out_, in_, flags, initial, width, n=C, backward=False):
                order = slice(None, None, -1) if backward else slice(None)
                for f in range(width) if isinstance(width, int) else width:
                    last = dve.tensor_tensor_scan(out=out_[:, order, f], data0=flags[:, order], data1=in_[:, order, f],
                                                  initial=initial[:, f:f + 1], op0=ALU.mult, op1=ALU.add)
                return last

            CD = C * D

            def wait_done(phase, i):
                dve.wait_ge(s_done, before[phase, "done"] + 1 + i)
                step(dve.memset(cols[:, SCR:SCR + 1], 0.0))

            def source_first(i, it, b):
                dve.wait_ge(s_ld[b], before["source", "ld"] + 16 * (it + 1))
                step(cast(TY[b], etf[:, bass.ds(i * C, C)]))
                ln = before["source", "ln"] + (1 if isinstance(i, int) and i == 0 else 2 * i)
                norm(XB[:, b, :], G[:, b, :], C, ln).then_inc(s_ready, 1)
                dve.wait_ge(s_ready, before["source", "ready"] + 1 + i)
                step(dve.memset(col(SCR), 0.0))

            def source(i, it, b, next_it=None):
                step.reset()
                for q in range(PAIRS):
                    dve.wait_ge(s_turnedh, i * PAIRS + q + 1)
                    dve.wait_ge(s_mmult, i * PAIRS + q + 1)
                    for r in range(RELS // 2):
                        last = dve.scalar_tensor_tensor(out=MASKED[q % 2][:, r * 256:(r + 1) * 256], in0=PS[:, q % 2, 256:512],
                                                        scalar=relc[:, r:r + 1], in1=AT[:, q % 2, 0:256], op0=ALU.is_equal, op1=ALU.mult)
                    last.then_inc(s_mask, 1)
                if next_it is not None:
                    source_first(i + 1, next_it, 1 - b)
                dve.wait_ge(s_lput, before["source", "lone"] + CREDIT + len(SRC_UNITS) * (i + 1))
                step(tt(XB[:, b, :], XB[:, b, :], O[:, b, 0:CD], ALU.add))
                ln = before["source", "ln"] + (2 * i + 3 if next_it is not None else 2 * i + 2)
                step(norm(XB[:, b, :], O[:, b, 0:CD], C, ln))
                dve.wait_ge(s_mout, AHEAD + GROUPS * (i + 1))
                scans(cut(R[:, b, CD:]), cut(R[:, b, 0:CD]), same[:, bass.ds(i * C, C)], R[:, 1 - b, 2 * CD - D:2 * CD], D).then_inc(s_done, 1)
                wait_done("source", i)

            dve.sem_inc(s_mask, AHEAD)
            source_first(0, 0, 0)
            with dve.Fori(0, TURNS - 1) as it:
                source(2 * it, it, 0, it)
                source(2 * it + 1, it, 1, it + 1)
            source(CHUNKS - 2, TURNS - 1, 0, TURNS - 1)
            source(CHUNKS - 1, TURNS - 1, 1)
            step.reset()
            dve.wait_ge(s_carry, 1)
            step(cast(VB[:], PS[:, 5, 0:D]))
            barrier()

            def dest(i, it, b):
                step.reset()
                dve.wait_ge(s_ld[b], before["dest", "ld"] + 32 * (it + 1))
                step(tt(cut(SQ[:]), VB[:].unsqueeze(1).broadcast_to([P, C, D]), over(first_tail[:, bass.ds(i * C, C)], D), ALU.mult))
                step(tt(XB[:, b, :], XB[:, b, :], R[:, b, 0:CD], ALU.add))
                step(tt(XB[:, b, :], XB[:, b, :], SQ[:], ALU.add))
                norm(XB[:, b, :], G[:, b, :], C, before["dest", "ln"] + 1 + i).then_inc(s_done, 1)
                wait_done("dest", i)

            paired(dve, TURNS, dest)
            barrier()

            def nodes_first(i, turn, j):
                dve.wait_ge(s_xn[j], 16 * (turn + 1))
                step(dve.memset(col(SCR), 0.0))
                norm(XN[j], G[0:NP_, j % 2, 0:NC * D], NC, before["nodes", "ln"] + 1 + i, NP_).then_inc(s_ready, 1)

            def nodes_last(i, half, j):
                dve.wait_ge(s_st[j % 2], before["nodes", "st"] + 16 * half)
                step(dve.memset(col(SCR), 0.0))
                dve.wait_ge(s_lput, before["nodes", "lone"] + CREDIT + len(NODE_UNITS) * (i + 1))
                tt(R[0:NP_, j % 2, 0:NC * D], XN[j], O[0:NP_, j % 2, 0:NC * D], ALU.add).then_inc(s_done, 1)
                wait_done("nodes", i)

            nodes_first(0, 0, 0)
            with dve.Fori(0, NCHUNKS // 4 - 1) as it:
                for j in range(4):
                    step.reset()
                    nodes_first(4 * it + j + 1, it + (j + 1) // 4, (j + 1) % 4)
                    nodes_last(4 * it + j, 2 * it + j // 2, j)
            for j in range(4):
                if j < 3:
                    nodes_first(NCHUNKS - 4 + j + 1, NCHUNKS // 4 - 1, j + 1)
                nodes_last(NCHUNKS - 4 + j, NCHUNKS // 2 - 2 + j // 2, j)
            step.reset()
            barrier()
            dve.wait_ge(s_infoc, 1)
            step(ts(tmp[:], EE[:, 0, :], 0.0, FAR, ALU.is_equal, ALU.mult))
            step(ts(EE[:, 0, :], EE[:, 0, :], 1.0, None, ALU.subtract))
            step(tt(tmp[:], tmp[:], EE[:, 0, :], ALU.add))
            step(cast(srcq[:], tmp[:]))
            step(cast(EE[:, 2, :], dsti[:]))
            step(tt(EE[:, 2, :], EE[:, 2, :], tail[:], ALU.mult))
            step(dve.scalar_tensor_tensor(out=EE[:, 2, :], in0=rest[:], scalar=FAR, in1=EE[:, 2, :], op0=ALU.mult, op1=ALU.add))
            step(cast(dstq[:], EE[:, 2, :]))
            step(ts(EE[:, 1, :], EE[:, 1, :], 1.0, None, ALU.max))
            ts(EE[:, 5, :], EE[:, 5, :], 1.0, None, ALU.max).then_inc(s_prep, 1)
            dve.wait_ge(s_patch, 16)
            step(ts(cols[:, SCR:SCR + 1], PG[:, 0, 0:1], 1.0, 0.0, ALU.subtract, ALU.max))
            cast(coli(IX_LAST), cols[:, SCR:SCR + 1]).then_inc(s_last, 1)
            dve.wait_ge(s_prep, 2)
            step(dve.reciprocal(rs_src[:], rs_src[:]))
            step(dve.reciprocal(rs_dst[:], rs_dst[:]))
            for values, k in ((rs_dst, RSDST_FT),):
                step(tt(tmp[:], values[:], first_tail[:], ALU.mult))
                step(dve.tensor_reduce(col(k), tmp[:], AX_X, ALU.add))
            step(ts(col(SCR), col(SCR), 1.0, -1.0, ALU.min, ALU.add))
            tt(col(SCR), col(SCR), bias1c[:], ALU.max).then_inc(s_prep, 1)
            dve.wait_ge(s_carry, before["prep", "carry"] + 1)
            step(cast(cut(XC[:]), PS[:, 3, 0:D].unsqueeze(1).broadcast_to([P, C, D])))
            dve.nop().then_inc(s_prep, 1)
            barrier()

            def halves(b, n):
                both = cut(HH[:, b, 0:n * D2], D2)
                return both[:, :, 0:D], both[:, :, D:]

            def per_row(array, i, first, n):
                return over(array[:, bass.ds(i * C, C)] if n == C else col(first), D)

            def operands(k, i, b, n):
                r, (left, right) = cut(R[:, b, 0:n * D]), halves(b, n)
                if k < 3:
                    return tt(left, r, per_row(inv_in, i, INV_FT, n), ALU.mult)
                step(tt(right, right, per_row(rs_dst, i, RSDST_FT, n), ALU.mult))
                step(tt(right, right, r, ALU.mult))
                return cast(left, r)

            def new_state(k, layer, i, b, n):
                o, xb = O[:, b, 0:n * D], XB[:, b, 0:n * D]
                if k == 3:
                    step(tt(cut(o), cut(o), per_row(rs_in, i, RSIN_FT, n), ALU.mult))
                else:
                    step(tt(cut(o), cut(o), lastb[:].unsqueeze(1).broadcast_to([P, n, D]), ALU.add))
                step(tt(xb, xb, o, ALU.add))
                norm(xb, o, n, before[layer, "ln"] + 1 + i).then_inc(s_done, 1)

            for b in range(2):
                dve.sem_inc(s_tot[b], 16)
            for k, layer in enumerate(LAYERS):
                normed = k >= 2

                def gathered(i, it, b):
                    step.reset()
                    dve.wait_ge(s_tot[b], before[layer, "tot"] + 16 * (it + 1))
                    step(dve.memset(col(SCR), 0.0))
                    dve.wait_ge(s_g[b], before[layer, "gath"] + 16 * C * (it + 1))
                    if k == 3:
                        step(tt(cut(G[:, b, :]), cut(G[:, b, :]), over(rs_src[:, bass.ds(i * C, C)], D), ALU.mult))
                    scans(cut(R[:, b, 0:CD]), cut(G[:, b, :]), same[:, bass.ds(i * C, C)], R[:, 1 - b, CD - D:CD], D).then_inc(s_scan, 1)

                def state(i, it, b):
                    dve.wait_ge(s_scan, before[layer, "scan"] + 1 + i)
                    step(dve.memset(col(SCR), 0.0))
                    dve.wait_ge(s_ld[b], before[layer, "ld"] + (1 + normed) * 16 * (it + 1))
                    operands(k, i, b, C).then_inc(s_ready, 1)

                def finish(i, it, b):
                    dve.wait_ge(s_out, before[layer, "group"] + AHEAD + GROUPS * (i + 1))
                    new_state(k, layer, i, b, C)

                if normed:
                    gathered(0, 0, 0)
                    state(0, 0, 0)

                    def turn(i, it, b, next_it):
                        gathered(i + 1, next_it, 1 - b)
                        finish(i, it, b)
                        state(i + 1, next_it, 1 - b)

                    with dve.Fori(0, TURNS - 1) as it:
                        turn(2 * it, it, 0, it)
                        turn(2 * it + 1, it, 1, it + 1)
                    turn(CHUNKS - 2, TURNS - 1, 0, TURNS - 1)
                    finish(CHUNKS - 1, TURNS - 1, 1)
                else:
                    def turn(i, it, b):
                        gathered(i, it, b)
                        state(i, it, b)

                    paired(dve, TURNS, turn)
                step.reset()
                barrier()
                dve.wait_ge(s_patch, before[layer, "patch"] + 16 * (2 + normed))
                dve.wait_ge(s_carry, before[layer, "carry"] + 1)
                step(tt(R[:, 0, 0:D], R[:, 0, 0:D], PS[:, 3, 0:D], ALU.add))
                operands(k, CHUNKS, 0, 1).then_inc(s_ready, 1)
                if normed:
                    dve.wait_ge(s_out, before[layer, "group"] + AHEAD + GROUPS * CHUNKS + 1)
                    new_state(k, layer, CHUNKS, 0, 1)
                barrier()

            def softmax(heads, X, Y, Z, at):
                pen_f, pen_b, pen = O[:, 0, 0:TILES], O[:, 0, TILES:2 * TILES], O[:, 0, 2 * TILES:3 * TILES]
                step(ts(pen_f, same[:], BIG, -BIG, ALU.mult, ALU.add))
                step(ts(pen_b, rest[:], BIG, -BIG, ALU.mult, ALU.add))
                for h in range(heads):
                    step(dve.tensor_tensor_scan(out=Y[:, h, :], data0=pen_f, data1=X[:, h, :], initial=-BIG, op0=ALU.add, op1=ALU.max))
                    step(dve.tensor_tensor_scan(out=Z[:, h, ::-1], data0=pen_b[:, ::-1], data1=X[:, h, ::-1], initial=-BIG, op0=ALU.add, op1=ALU.max))
                step(cast(tz[:, 0, 0:heads], Y[:, 0:heads, TILES - 1]))
                cast(tz[:, 1, 0:heads], Z[:, 0:heads, 0]).then_inc(s_sm, 1)
                dve.wait_ge(s_sm, at + 2)
                row = lambda k: rowz[0:heads, k, :]
                step(cast(rowz[0:heads, 4:6, :].rearrange("h k p -> h (k p)"), PS[0:heads, 0, 0:2 * P]))
                step(dve.tensor_tensor_scan(out=row(6), data0=row(0), data1=row(4), initial=-BIG, op0=ALU.add, op1=ALU.max))
                step(dve.tensor_tensor_scan(out=row(7)[:, ::-1], data0=row(1)[:, ::-1], data1=row(5)[:, ::-1], initial=-BIG, op0=ALU.add, op1=ALU.max))
                step(dve.memset(rowz[0:heads, 4:6, :], -BIG))
                step(tt(row(4)[:, 1:], row(6)[:, 0:P - 1], row(2)[:, 1:], ALU.add))
                tt(row(5)[:, 0:P - 1], row(7)[:, 1:], row(3)[:, 0:P - 1], ALU.add).then_inc(s_sm, 1)
                dve.wait_ge(s_sm, at + 4)
                step(cast(tz[:, 2:4, 0:heads], PS[:, 1, 0:2 * HEADS].rearrange("p (k h) -> p k h", k=2)[:, :, 0:heads]))
                step(tt(Y[:, 0:heads, :], Y[:, 0:heads, :], Z[:, 0:heads, :], ALU.max))
                for seg, k in ((first_seg, 2), (last_seg, 3)):
                    step(ts(pen, seg[:], BIG, -BIG, ALU.mult, ALU.add))
                    for h in range(heads):
                        step(dve.scalar_tensor_tensor(out=Y[:, h, :], in0=pen, scalar=tz[:, k, h:h + 1], in1=Y[:, h, :], op0=ALU.add, op1=ALU.max))
                tt(X[:, 0:heads, :], X[:, 0:heads, :], Y[:, 0:heads, :], ALU.subtract).then_inc(s_sm, 1)
                dve.wait_ge(s_sm, at + 6)
                for h in range(heads):
                    step(dve.tensor_tensor_scan(out=Z[:, h, :], data0=same[:], data1=X[:, h, :], initial=0.0, op0=ALU.mult, op1=ALU.add))
                cast(tz[:, 4, 0:heads], Z[:, 0:heads, TILES - 1]).then_inc(s_sm, 1)
                dve.wait_ge(s_sm, at + 8)
                step(cast(tz[:, 6, 0:heads], PS[:, 2, 0:heads]))
                for h in range(heads):
                    step(dve.scalar_tensor_tensor(out=Z[:, h, :], in0=first_seg[:], scalar=tz[:, 6, h:h + 1], in1=Z[:, h, :], op0=ALU.mult, op1=ALU.add))
                step(ts(Z[:, 0:heads, :], Z[:, 0:heads, :], 1e-16, None, ALU.add))
                step(dve.reciprocal(Z[:, 0:heads, :], Z[:, 0:heads, :]))
                step(tt(Y[:, 0:heads, :], Z[:, 0:heads, :], first_tail[:].unsqueeze(1).broadcast_to([P, heads, TILES]), ALU.mult))
                step(dve.tensor_reduce(tz[:, 5, 0:heads], Y[:, 0:heads, :], AX_X, ALU.add))

            def back(i):
                return i * (-1) + (CHUNKS - 1)

            dve.wait_ge(s_patch, before["att1", "patch"] + 16)
            step(cast(HH[:, 1, D:D2], VB[:]))

            def spread(phase, i, it, b, to, initial):
                dve.wait_ge(s_ld[b], before[phase, "ld"] + 16 * (it + 1))
                at = bass.ds(back(i) * C, C)
                step(tt(cut(XB[:, b, :]), cut(XB[:, b, :]), over(tail[:, at], D), ALU.mult))
                step(cast(st[:, 0, :], rest[:, at]))
                return scans(to, cut(XB[:, b, :]), st[:, 0, :], initial, D, backward=True)

            def operands1(i, it, b):
                step.reset()
                spread("att1", i, it, b, halves(b, C)[1], HH[:, 1 - b, D:D2]).then_inc(s_ready, 1)
                dve.wait_ge(s_ready, before["att1", "ready"] + 1 + i)
                step(dve.memset(col(SCR), 0.0))

            def scores1(i, it, b):
                dve.wait_ge(s_st[b], before["att1", "st"] + 16 * it)
                step(dve.memset(col(SCR), 0.0))
                for g in range(GROUPS):
                    k = (g + b * GROUPS) % 2
                    at = before["att1", "group"] + GROUPS * i + g
                    dve.wait_ge(s_sums, GROUPS * i + g + 1)
                    dve.scalar_tensor_tensor(out=SX[:, k, 0:512], in0=SX[:, k, 0:512], scalar=0.2, in1=SX[:, k, 0:512],
                                             op0=ALU.mult, op1=ALU.max).then_inc(s_leaky, 1)
                    dve.wait_ge(s_mult, at + 1 + AHEAD)
                    tt(cut(O[:, b, g * 512:(g + 1) * 512], D2), cut(PS[:, 6 + k, :], D2), bl1b[:].unsqueeze(1).broadcast_to([P, G4, D2]),
                       ALU.add).then_inc(s_out, 1)
                dve.wait_ge(s_scored, GROUPS * i + GROUPS)
                step(cast(Ea[:, :, bass.ds(back(i) * C, C)].rearrange("p h j -> p j h"), cut(PS[:, 2 + b, 0:C * HEADS], HEADS)))

            operands1(0, 0, 0)
            with dve.Fori(0, TURNS - 1) as it:
                operands1(2 * it + 1, it, 1)
                scores1(2 * it, it, 0)
                operands1(2 * it + 2, it + 1, 0)
                scores1(2 * it + 1, it, 1)
            operands1(CHUNKS - 1, TURNS - 1, 1)
            scores1(CHUNKS - 2, TURNS - 1, 0)
            scores1(CHUNKS - 1, TURNS - 1, 1)
            step.reset()
            barrier()
            softmax(HEADS, Ea, Eb, Ec, 0)
            barrier()

            def weighted(i, it, b, between=None):
                step.reset()
                dve.wait_ge(s_ld[b], before["sum1", "ld"] + 16 * (it + 1))
                at = bass.ds(i * C, C)
                rows4 = lambda t: t.rearrange("p (j h c) -> p j h c", h=HEADS, c=D2 // HEADS)
                per_head = lambda e: e[:, :, at].rearrange("p h j -> p j h").unsqueeze(3).broadcast_to([P, C, HEADS, D2 // HEADS])
                step(tt(rows4(XL[b]), rows4(XL[b]), per_head(Ea), ALU.mult))
                for g in range(GROUPS):
                    fs = range(g * D2 // GROUPS, (g + 1) * D2 // GROUPS)
                    last = scans(cut(R[:, b, :], D2), cut(XL[b], D2), same[:, at], R[:, 1 - b, 2 * CD - D2:], fs)
                    if g == GROUPS - 1:
                        last.then_inc(s_scan, 1)
                    if between:
                        between(g)
                dve.wait_ge(s_scan, before["sum1", "scan"] + 1 + i)
                tt(rows4(HH[:, b, :]), rows4(R[:, b, :]), per_head(Ec), ALU.mult).then_inc(s_ready, 1)

            def elu(i, b, g, n=G4):
                k = (g + b * GROUPS) % 2
                at = GROUPS * i + g
                dve.wait_ge(s_exp, at + 1)
                step(ts(SX[:, k, 0:n * P], SX[:, k, 0:n * P], 1.0, -1.0, ALU.min, ALU.add))
                dve.wait_ge(s_mult, before["sum1", "group"] + GROUPS * i + g + 1)
                dve.scalar_tensor_tensor(out=AT[:, k, 0:n * P], in0=PS[:, 4 + k, 0:n * P], scalar=bias1c[:], in1=SX[:, k, 0:n * P],
                                         op0=ALU.add, op1=ALU.max).then_inc(s_elu, 1)

            def elus(i, b):
                return lambda g: elu(i, b, g)

            dve.sem_inc(s_elu, AHEAD)
            weighted(0, 0, 0)
            with dve.Fori(0, TURNS - 1) as it:
                weighted(2 * it + 1, it, 1, elus(2 * it, 0))
                weighted(2 * it + 2, it + 1, 0, elus(2 * it + 1, 1))
            weighted(CHUNKS - 1, TURNS - 1, 1, elus(CHUNKS - 2, 0))
            for g in range(GROUPS):
                elu(CHUNKS - 1, 1, g)
            step.reset()
            barrier()
            dve.wait_ge(s_patch, before["sum1", "patch"] + 16)
            dve.wait_ge(s_carry, before["sum1", "carry"] + 1)
            step(tt(R[:, 0, 0:D2], R[:, 0, 0:D2], PS[:, 3, 0:D2], ALU.add))
            tt(cut(HH[:, 0, 0:D2], D2 // HEADS), cut(R[:, 0, 0:D2], D2 // HEADS), over(tz[:, 5, :], D2 // HEADS), ALU.mult).then_inc(s_ready, 1)
            elu(CHUNKS, 0, 0, 1)
            barrier()

            dve.wait_ge(s_patch, before["att2", "patch"] + 16)
            step(cast(HH[:, 1, 0:D], VB[:]))

            def scores2(i, it, b):
                step.reset()
                one, two = HH[:, b, 0:CD], HH[:, b, CD:]
                spread("att2", i, it, b, cut(one), HH[:, 1 - b, 0:D]).then_inc(s_scan2, 1)
                dve.wait_ge(s_g[b], before["att2", "gath"] + 16 * C * (it + 1))
                step(dve.memset(col(SCR), 0.0))
                dve.wait_ge(s_scan2, i + 1)
                step(tt(two, G[:, b, :], one, ALU.add))
                step(dve.scalar_tensor_tensor(out=two, in0=two, scalar=0.2, in1=two, op0=ALU.mult, op1=ALU.max))
                step(tt(cut(two), cut(two), attb2[:].unsqueeze(1).broadcast_to([P, C, D]), ALU.mult))
                dve.tensor_reduce(Eb[:, 0, bass.ds(back(i) * C, C)], cut(two), AX_X, ALU.add).then_inc(s_done, 1)

            paired(dve, TURNS, scores2)
            step.reset()
            barrier()
            softmax(1, Eb, Ea, Ec, 8)
            barrier()

            def result(r, o, xb, n, inverse):
                step(tt(cut(o), cut(r), inverse, ALU.mult))
                step(tt(cut(o), cut(o), bias2b[:].unsqueeze(1).broadcast_to([P, n, D]), ALU.add))
                return tt(o, o, xb, ALU.add)

            def weighted2(i, it, b):
                step.reset()
                dve.wait_ge(s_ld[b], before["sum2", "ld"] + 32 * (it + 1))
                at = bass.ds(i * C, C)
                step(tt(cut(G[:, b, :]), cut(G[:, b, :]), over(Eb[:, 0, at], D), ALU.mult))
                scans(cut(R[:, b, 0:CD]), cut(G[:, b, :]), same[:, at], R[:, 1 - b, CD - D:CD], D).then_inc(s_scan, 1)
                dve.wait_ge(s_scan, before["sum2", "scan"] + 1 + i)
                result(R[:, b, 0:CD], O[:, b, 0:CD], XB[:, b, :], C, over(Ec[:, 0, at], D)).then_inc(s_ready, 1)

            paired(dve, TURNS, weighted2)
            step.reset()
            barrier()
            dve.wait_ge(s_patch, before["sum2", "patch"] + 32)
            dve.wait_ge(s_carry, before["sum2", "carry"] + 1)
            step(tt(R[:, 0, 0:D], R[:, 0, 0:D], PS[:, 3, 0:D], ALU.add))
            result(R[:, 0, 0:D], O[:, 0, 0:D], XB[:, 0, 0:D], 1, over(tz[:, 5, 0:1], D)).then_inc(s_sm, 1)
            barrier()

        @block.tensor
        def _(pe):
            barrier = Barrier(pe)
            pe.wait_ge(s_const, 2)
            pe.wait_ge(s_keys, 1)
            pe.wait_ge(s_cols, 1)
            pe.matmul(PS[:, 0, 0:P], cols[:, DF:DF + 1].broadcast_to([P, P]), ident[:], start=True, stop=True).then_inc(s_trans, 1)
            pe.wait_ge(s_w, 16 * WEIGHT_LOADS)
            pe.transpose(PS[:, 1, 0:P], SQ[:, 0:D2], ident[:]).then_inc(s_trans, 1)
            pe.transpose(PS[:, 1, P:2 * P], SQ[:, D2:2 * D2], ident[:]).then_inc(s_trans, 1)
            for k, c in enumerate((PEN_P, PEN_N, CAP_P, CAP_N)):
                pe.matmul(PS[0:HEADS, 2, k * P:(k + 1) * P], cols[:, c:c + 1].broadcast_to([P, HEADS]), ident[:],
                          start=True, stop=True).then_inc(s_trans, 1)
            pe.wait_ge(s_keys, 2)
            pe.matmul(PS[:, 3, 0:1], CARRY[:], inv_in[:, TILES - 1:TILES], start=True, stop=True).then_inc(s_trans, 1)
            barrier()
            for k in range(3 * LOB):
                pe.matmul(PS[:, k, 0:HI + 1], zeroh[:, 0:P], zeroh[:, 0:HI + 1], start=True, stop=False, skip_group_check=True)
            pe.matmul(PS[:, 6, 0:1], zeroh[:, 0:P], zeroh[:, 0:1], start=True, stop=True).then_inc(s_binned, 2)
            Rh = R[:, :, :].bitcast(F16)
            h1 = HI + 1
            with pe.Fori(0, HTURNS) as it:
                for b in range(2):
                    hot = Rh[:, b, 0:HCOLS * HSLOT].rearrange("p (k s) -> p k s", k=HCOLS)
                    pe.wait_ge(s_hot, 2 * it + b + 1)
                    for k in range(HCOLS):
                        o = hot[:, k, :]
                        for l in range(LOB):
                            lo_src = o[:, 3 * h1 + l * P:3 * h1 + (l + 1) * P]
                            lo_dst = o[:, 3 * h1 + 256 + l * P:3 * h1 + 256 + (l + 1) * P]
                            pe.matmul(PS[:, l, 0:h1], lo_src, o[:, 0:h1], start=False, stop=False, skip_group_check=True)
                            pe.matmul(PS[:, LOB + l, 0:h1], lo_dst, o[:, h1:2 * h1], start=False, stop=False, skip_group_check=True)
                            last = pe.matmul(PS[:, 2 * LOB + l, 0:h1], lo_dst, o[:, 2 * h1:3 * h1], start=False, stop=False, skip_group_check=True)
                    last.then_inc(s_binned, 1)
            for k in range(3 * LOB):
                last = pe.matmul(PS[:, k, 0:HI + 1], zeroh[:, 0:P], zeroh[:, 0:HI + 1], start=False, stop=True, skip_group_check=True)
            last.then_inc(s_binned, 1)
            barrier()

            def lone_unit(phase, units, ring, first_bank, arrays, parts, i, b, n):
                unit = stage, k, g = units[n]
                base = before[phase, "lone"] + len(units) * i
                width = 2 * parts
                bank = first_bank + (n + b * len(units)) % ring
                at = arrays[(g + b * (len(units) % 2)) % 2]
                pe.wait_ge(s_lput, base + n + 1 - ring + CREDIT)
                if stage == "turn":
                    pe.wait_ge(s_ready, before[phase, "ready"] + 1 + i)
                    for q in range(2):
                        last = pe.transpose(PS[:, bank, q * parts:(q + 1) * parts],
                                            G[0:parts, b, (2 * g + q) * D2:(2 * g + q + 1) * D2], ident[0:parts, 0:parts])
                else:
                    pe.wait_ge(s_lput, base + units.index(made_from(unit)) + 1 + CREDIT)
                    if stage == "step":
                        last = pe.matmul(PS[:, bank, 0:width], WS[:, k, :], at[:, k * 256:k * 256 + width], start=True, stop=True,
                                         skip_group_check=True)
                    else:
                        for q in range(2):
                            last = pe.transpose(PS[0:parts, bank, q * P:(q + 1) * P],
                                                at[:, (k + 1) * 256 + q * parts:(k + 1) * 256 + (q + 1) * parts], ident[:])
                last.then_inc(s_lmade, 1)

            pe.sem_inc(s_mult, AHEAD)
            pe.sem_inc(s_mmult, AHEAD)

            def spread(i, b, q):
                pe.wait_ge(s_ready, before["source", "ready"] + 1 + i)
                pe.wait_ge(s_mask, i * PAIRS + q + 1)
                for j in range(2):
                    at = 2 * q + j
                    for r in range(2):
                        pe.matmul(PS[r * D:(r + 1) * D, q % 2, j * P:(j + 1) * P], G[:, b, at * D:(at + 1) * D], ident[:],
                                  start=True, stop=True, skip_group_check=True)
                    last = pe.matmul(PS[:, q % 2, 256 + j * P:256 + (j + 1) * P], TY[b][:, at:at + 1].broadcast_to([P, P]), ident[:],
                                     start=True, stop=True, skip_group_check=True)
                last.then_inc(s_spread, 1)

            def message(i, b, q):
                pe.wait_ge(s_mask, i * PAIRS + q + 1 + AHEAD)
                g = q // 2
                if q % 2 == 0:
                    pe.wait_ge(s_mout, i * GROUPS + g + 1)
                for j in range(2):
                    to = PS[:, 2 + (g + b) % 2, (2 * (q % 2) + j) * D:(2 * (q % 2) + j + 1) * D]
                    for r in range(RELS // 2):
                        last = pe.matmul(to, MASKED[q % 2][:, r * 256 + j * P:r * 256 + (j + 1) * P], W0[:, r, :], start=(r == 0),
                                         stop=(r == RELS // 2 - 1), skip_group_check=True)
                last.then_inc(s_mmult, 1)

            def source(i, it, b):
                for q in range(2):
                    spread(i, b, q)
                for n in range(len(SRC_UNITS)):
                    lone_unit("source", SRC_UNITS, SRC_RING, 6, SRC_AT, P, i, b, n)
                for q in range(PAIRS):
                    message(i, b, q)
                    if q + 2 < PAIRS:
                        spread(i, b, q + 2)

            paired(pe, TURNS, source)
            pe.wait_ge(s_done, before["source", "done"] + CHUNKS)
            pe.matmul(PS[:, 5, 0:D], CARRY[:], R[:, 1, 2 * C * D - D:2 * C * D], start=True, stop=True).then_inc(s_carry, 1)
            barrier()
            barrier()
            def nodes(i, it, b):
                for n in range(len(NODE_UNITS)):
                    lone_unit("nodes", NODE_UNITS, NODE_RING, 0, NODE_AT, NP_, i, b, n)

            paired(pe, NCHUNKS // 2, nodes)
            barrier()
            pe.wait_ge(s_prep, 3)
            pe.matmul(PS[:, 3, 0:D], cols[:, SCR:SCR + 1].broadcast_to([P, P]), WG2[:, 0:D], start=True, stop=False)
            pe.matmul(PS[:, 3, 0:D], ones[:], BG2[:, 0:D], start=False, stop=True).then_inc(s_carry, 1)
            barrier()

            def turn(phase, i, b, g, n=G4, freed=None):
                pe.wait_ge(s_ready, before[phase, "ready"] + 1 + i)
                if 2 <= g < GROUPS:
                    pe.wait_ge(*(freed(i, g - 2) if freed else (s_copied, before[phase, "group"] + GROUPS * i + g - 1)))
                k = (g + b * GROUPS) % 2
                for q in range(n):
                    last = pe.transpose(PS[:, 4 + k, q * P:(q + 1) * P], HH[:, b, (g * G4 + q) * D2:(g * G4 + q + 1) * D2], ident[:])
                last.then_inc(s_turned, 1)

            def multiply(phase, i, b, g, weights, bias, width, n=G4, to_bank=None, ready=None):
                k = (g + b * GROUPS) % 2
                at = before[phase, "group"] + GROUPS * i + g
                if ready is None:
                    pe.wait_ge(s_copied, before[phase, "group"] + GROUPS * i + g + 1)
                else:
                    pe.wait_ge(*ready(i, g))
                pe.wait_ge(s_out, at + 1)
                for q in range(n):
                    if width == 2 * D2:
                        to = PS[:, 2 * k + q // 2, (q % 2) * width:(q % 2 + 1) * width]
                    else:
                        to = PS[:, 6 + k, q * width:(q + 1) * width]
                    last = pe.matmul(to, AT[:, k, q * P:(q + 1) * P], weights, start=True, stop=bias is None, skip_group_check=True)
                    if bias is not None:
                        last = pe.matmul(to, ones[:], bias, start=False, stop=True, skip_group_check=True)
                last.then_inc(s_mult, 1)

            def products(phase, *how, **more):
                def body(i, it, b):
                    for g in range(GROUPS + 2):
                        if g < GROUPS:
                            turn(phase, i, b, g, freed=more.get("ready"))
                        if g >= 2:
                            multiply(phase, i, b, g - 2, *how, **more)
                return body

            def carry(phase, width, at):
                pe.matmul(PS[:, 3, 0:width], CARRY[:], R[:, 1, at - width:at], start=True, stop=True).then_inc(s_carry, 1)

            for k, layer in enumerate(LAYERS):
                how = (WD[:, k, :], BS[:, k, 0:D], D) if k < 2 else (WD[:, k, :] if k == 2 else W12[:], None, D)
                paired(pe, TURNS, products(layer, *how))
                barrier()
                carry(layer, D, C * D)
                turn(layer, CHUNKS, 0, 0, 1)
                multiply(layer, CHUNKS, 0, 0, *how, n=1)
                barrier()
            def sums1(i, b, g):
                k = (g + b * GROUPS) % 2
                at = before["att1", "group"] + GROUPS * i + g
                pe.wait_ge(s_copied, at + 1)
                pe.wait_ge(s_out, at + 1)
                pe.matmul(PS[:, k, :], WG1[:, 0:D2], AT[:, k, :], start=True, stop=True, skip_group_check=True)
                for q in range(G4):
                    last = pe.matmul(PS[:, 6 + k, q * P:(q + 1) * P], AT[:, k, q * P:(q + 1) * P], WG1[:, D2:], start=True, stop=True,
                                     skip_group_check=True)
                last.then_inc(s_mult, 1)

            def scored1(i, b, g):
                k = (g + b * GROUPS) % 2
                pe.wait_ge(s_leaky, GROUPS * i + g + 1)
                for q in range(G4):
                    at = (g * G4 + q) * HEADS
                    last = pe.matmul(PS[:, 2 + b, at:at + HEADS], SX[:, k, q * P:(q + 1) * P], ATTD[:], start=True, stop=True,
                                     skip_group_check=True)
                last.then_inc(s_scored, 1)

            def scores1(i, it, b):
                pe.wait_ge(s_left, 1 + i)
                for g in range(GROUPS + 3):
                    if g < GROUPS:
                        turn("att1", i, b, g)
                    if 2 <= g < GROUPS + 2:
                        sums1(i, b, g - 2)
                    if g >= 3:
                        scored1(i, b, g - 3)

            paired(pe, TURNS, scores1)
            barrier()

            def softmax(heads, at):
                pe.wait_ge(s_sm, at + 1)
                for k in range(2):
                    last = pe.transpose(PS[0:heads, 0, k * P:(k + 1) * P], tz[:, k, 0:heads], ident[:])
                last.then_inc(s_sm, 1)
                pe.wait_ge(s_sm, at + 3)
                for k in range(2):
                    last = pe.transpose(PS[:, 1, k * HEADS:k * HEADS + heads], rowz[0:heads, 4 + k, :], ident[0:heads, 0:heads])
                last.then_inc(s_sm, 1)
                pe.wait_ge(s_sm, at + 7)
                pe.matmul(PS[:, 2, 0:heads], CARRY[:], tz[:, 4, 0:heads], start=True, stop=True).then_inc(s_sm, 1)

            softmax(HEADS, 0)
            barrier()
            how = (WG2[:], BG2[:], D2)
            ready = lambda i, g: (s_elu, GROUPS * i + g + 1 + AHEAD)
            paired(pe, TURNS, products("sum1", *how, ready=ready))
            barrier()
            carry("sum1", D2, 2 * C * D)
            turn("sum1", CHUNKS, 0, 0, 1)
            multiply("sum1", CHUNKS, 0, 0, *how, n=1, ready=ready)
            barrier()
            barrier()
            softmax(1, 8)
            barrier()
            barrier()
            carry("sum2", D, C * D)
            barrier()

        @block.scalar
        def _(act):
            barrier = Barrier(act)
            act.wait_ge(s_keys, 3)
            act.activation(rs_in[:], inv_in[:], ACT.Sqrt).then_inc(s_trans, 1)
            barrier()
            barrier()

            def square(n, ln, parts=P):
                act.wait_ge(s_xc, ln)
                act.activation(SQ[0:parts, 0:n * D], XC[0:parts, 0:n * D], ACT.Square).then_inc(s_sq, 1)

            def root(n, ln, parts=P):
                act.wait_ge(s_var, ln)
                act.activation(st[0:parts, 2, 0:n], st[0:parts, 1, 0:n], ACT.Sqrt, bias=epsc[0:parts, :], scale=1.0 / D).then_inc(s_std, 1)

            def norm(n, ln):
                square(n, ln)
                root(n, ln)

            def lone_unit(phase, units, ring, first_bank, arrays, parts, rows_to, i, b, n, last_bias=2):
                stage, k, g = units[n]
                width = 2 * parts
                bank = first_bank + (n + b * len(units)) % ring
                at = arrays[(g + b * (len(units) % 2)) % 2]
                act.wait_ge(s_lmade, before[phase, "lone"] + len(units) * i + n + 1)
                if stage == "turn":
                    last = act.copy(at[:, 0:width], PS[:, bank, 0:width])
                elif stage == "step":
                    last = act.activation(at[:, (k + 1) * 256:(k + 1) * 256 + width], PS[:, bank, 0:width],
                                          ACT.Relu if k < 2 else ACT.Identity, bias=bsc[:, k:k + 1] if k < 2 else bsc[:, last_bias:last_bias + 1])
                else:
                    last = act.copy(rows_to(k)[0:parts, g * 256:(g + 1) * 256], PS[0:parts, bank, 0:256])
                last.then_inc(s_lput, 1)

            act.sem_inc(s_out, AHEAD)
            act.sem_inc(s_mout, AHEAD)
            act.sem_inc(s_lput, CREDIT)

            def turned(i, q):
                act.wait_ge(s_spread, i * PAIRS + q + 1)
                act.wait_ge(s_mask, i * PAIRS + q + 1)
                act.copy(AT[:, q % 2, 0:256], PS[:, q % 2, 0:256]).then_inc(s_turnedh, 1)

            def messages(i, b, g):
                act.wait_ge(s_mmult, i * PAIRS + 2 * g + 2 + AHEAD)
                act.copy(R[:, b, g * 256:(g + 1) * 256], PS[:, 2 + (g + b) % 2, 0:256]).then_inc(s_mout, 1)

            EARLY, LATER = 8, 12

            def units(i, b, some):
                rows_to = lambda k: (HH[:, b, 0:C * D], HH[:, b, C * D:], O[:, b, 0:C * D])[k]
                for n in some:
                    lone_unit("source", SRC_UNITS, SRC_RING, 6, SRC_AT, P, rows_to, i, b, n)

            def source(i, it, b, more=True):
                units(i, b, range(LATER, len(SRC_UNITS)))
                for q in range(PAIRS):
                    if q + 2 < PAIRS:
                        turned(i, q + 2)
                    if q % 2:
                        messages(i, b, q // 2)
                ln = before["source", "ln"] + 2 * i
                if more:
                    norm(C, ln + 2)
                    for q in range(2):
                        turned(i + 1, q)
                    units(i + 1, 1 - b, range(EARLY))
                square(C, ln + 2 + more)
                if more:
                    units(i + 1, 1 - b, range(EARLY, LATER))
                root(C, ln + 2 + more)

            norm(C, before["source", "ln"] + 1)
            for q in range(2):
                turned(0, q)
            units(0, 0, range(LATER))
            paired(act, TURNS - 1, source)
            source(CHUNKS - 2, None, 0)
            source(CHUNKS - 1, None, 1, more=False)
            barrier()
            paired(act, TURNS, lambda i, it, b: norm(C, before["dest", "ln"] + 1 + i))
            barrier()
            def nodes(i, it, b, more=True):
                ln = before["nodes", "ln"] + 2 + i
                for n in range(len(NODE_UNITS)):
                    if more and n == 4:
                        square(NC, ln, NP_)
                    if more and n == 10:
                        root(NC, ln, NP_)
                    lone_unit("nodes", NODE_UNITS, NODE_RING, 0, NODE_AT, NP_, lambda k: O[:, b, 0:NC * D], i, b, n, last_bias=3)

            square(NC, before["nodes", "ln"] + 1, NP_)
            root(NC, before["nodes", "ln"] + 1, NP_)
            paired(act, NCHUNKS // 2 - 1, nodes)
            nodes(NCHUNKS - 2, None, 0)
            nodes(NCHUNKS - 1, None, 1, more=False)
            barrier()
            act.wait_ge(s_prep, 1)
            act.activation(rs_src[:], EE[:, 1, :], ACT.Sqrt)
            act.activation(rs_dst[:], EE[:, 5, :], ACT.Sqrt)
            act.wait_ge(s_last, 1)
            act.activation(cols[:, SCR:SCR + 1], bias1c[:], ACT.Exp).then_inc(s_prep, 1)
            barrier()

            def copy(phase, i, b, g, n=G4):
                k = (g + b * GROUPS) % 2
                at = before[phase, "group"] + GROUPS * i + g
                act.wait_ge(s_turned, at + 1)
                act.wait_ge(s_mult, at + 1)
                act.copy(AT[:, k, 0:n * P], PS[:, 4 + k, 0:n * P]).then_inc(s_copied, 1)

            def multiplied(phase, i, g):
                act.wait_ge(s_mult, before[phase, "group"] + GROUPS * i + g + 1 + AHEAD)

            def out_rows(func):
                def put(phase, i, b, g, n=G4):
                    k = (g + b * GROUPS) % 2
                    multiplied(phase, i, g)
                    act.activation(O[:, b, g * 256:g * 256 + n * D], PS[:, 6 + k, 0:n * D], func).then_inc(s_out, 1)
                return put

            def products(phase, first, put, after=None):
                def body(i, it, b):
                    for g in range(GROUPS + 2):
                        if g < GROUPS:
                            first(phase, i, b, g)
                        if g >= 2:
                            put(phase, i, b, g - 2)
                    if after:
                        after(i)
                return body

            for k, layer in enumerate(LAYERS):
                put = out_rows(ACT.Relu if k < 2 else ACT.Identity)
                after = (lambda i, n=C: norm(n, before[layer, "ln"] + 1 + i)) if k >= 2 else None
                paired(act, TURNS, products(layer, copy, put, after))
                barrier()
                copy(layer, CHUNKS, 0, 0, 1)
                put(layer, CHUNKS, 0, 0, 1)
                if after:
                    after(CHUNKS, 1)
                barrier()

            def score_sums(phase, i, b, g):
                k = (g + b * GROUPS) % 2
                multiplied(phase, i, g)
                if isinstance(g, int) and g >= 2:
                    act.wait_ge(s_scored, GROUPS * i + g - 1)
                act.activation(SX[:, k, 0:512], PS[:, k, :], ACT.Identity, bias=blc[:, 0:1]).then_inc(s_sums, 1)

            put_scores = products("att1", copy, score_sums)

            def scores1(i, it, b):
                act.wait_ge(s_g[b], before["att1", "gath"] + 16 * C * (it + 1))
                act.copy(cut(HH[:, b, :], D2)[:, :, 0:D], cut(G[:, b, :])).then_inc(s_left, 1)
                put_scores(i, it, b)

            paired(act, TURNS, scores1)
            barrier()

            def softmax(X, heads, at):
                act.wait_ge(s_sm, at + 5)
                act.activation(X[:, 0:heads, :], X[:, 0:heads, :], ACT.Exp).then_inc(s_sm, 1)

            softmax(Ea, HEADS, 0)
            barrier()

            def exponential(phase, i, b, g, n=G4):
                k = (g + b * GROUPS) % 2
                act.wait_ge(s_turned, before[phase, "group"] + GROUPS * i + g + 1)
                act.wait_ge(s_elu, GROUPS * i + g + 1)
                act.activation(SX[:, k, 0:n * P], PS[:, 4 + k, 0:n * P], ACT.Exp, bias=bias1c[:]).then_inc(s_exp, 1)

            def second_operands(phase, i, b, g, n=G4, it=None):
                k = (g + b * GROUPS) % 2
                if g == 0 and it is not None:
                    act.wait_ge(s_rows[b], 32 * (it + 1))
                multiplied(phase, i, g)
                rows_ = cut(PS[:, 6 + k, 0:n * D2], D2)
                act.copy(cut(O[:, b, g * 256:g * 256 + n * D]), rows_[:, :, 0:D])
                act.copy(cut(O[:, b, C * D + g * 256:C * D + g * 256 + n * D]), rows_[:, :, D:]).then_inc(s_out, 1)

            for b in range(2):
                act.sem_inc(s_rows[b], 32)

            def both_steps(i, it, b):
                for g in range(GROUPS + 2):
                    if g < GROUPS:
                        exponential("sum1", i, b, g)
                    if g >= 2:
                        second_operands("sum1", i, b, g - 2, it=it)

            paired(act, TURNS, both_steps)
            barrier()
            exponential("sum1", CHUNKS, 0, 0, 1)
            second_operands("sum1", CHUNKS, 0, 0, 1)
            barrier()
            barrier()
            softmax(Eb, 1, 8)
            barrier()
            barrier()
            barrier()


_INS = ['x', 'src', 'dst', 'edge_type_16', 'L0_gnn_weight', 'L1_gnn_Wl', 'L1_gnn_Wr', 'L1_gnn_b',
        'L2_gnn_weight1', 'L2_gnn_weight2', 'L3_gnn_Wl1', 'L3_gnn_bl1', 'L3_gnn_Wr1', 'L3_gnn_br1',
        'L3_gnn_att1', 'L3_gnn_bias1', 'L3_gnn_Wl2', 'L3_gnn_bl2', 'L3_gnn_Wr2', 'L3_gnn_br2',
        'L3_gnn_att2', 'L3_gnn_bias2']


def kernel(**inputs):
    import concourse.bacc as bacc
    from concourse.bass_utils import run_bass_kernel_spmd

    nc = bacc.Bacc("TRN2", target_bir_lowering=False, num_devices=1)
    arrays, args = {}, []
    for name in _INS:
        a = np.ascontiguousarray(inputs[name])
        arrays[f"in_{name}"] = a
        args.append(nc.dram_tensor(f"in_{name}", a.shape, mybir.dt.from_np(a.dtype), kind="ExternalInput").ap())
    out = nc.dram_tensor("out_nodes", (N, D), F32, kind="ExternalOutput").ap()
    build_program(nc, *args, out)
    return run_bass_kernel_spmd(nc, [arrays], core_ids=[0]).results[0]["out_nodes"]
```
